# Optimizing a Trainium2 kernel written in Bass

```python
import numpy as np
import jax
import jax.numpy as jnp

def _softmax(x, axis=-1):
    return jax.nn.softmax(x, axis=axis)

def _gelu(x):
    return jax.nn.gelu(x, approximate=True)

def _silu(x):
    return jax.nn.silu(x)

def _sigmoid(x):
    return jax.nn.sigmoid(x)

def _layernorm(x, axis=-1, eps=1e-05):
    m = jnp.mean(x, axis=axis, keepdims=True)
    v = jnp.var(x, axis=axis, keepdims=True)
    return (x - m) / jnp.sqrt(v + eps)

def _scatter_add(tgt, idx, src, axis=0):
    return tgt.at[idx].add(src)

def _segment_sum(src, seg, n):
    return jax.ops.segment_sum(src, seg, n)
kernel_name = 'mk_adj_preln_d2_adj_r2_e0e623'

def setup_inputs(seed: int=0):
    np.random.seed(seed)
    _w = jnp.asarray

    def _rec_inputs():
        import jax
        import jax.numpy as jnp
        _gk = jax.random.key(seed)
        x = -0.0005963 + 1.001 * jax.random.normal(jax.random.fold_in(_gk, 1), (3327, 256), jnp.float32)
        _w = (1.0 + jnp.arange(3327, dtype=jnp.float32)) ** (-0.5)
        _w = _w / _w.mean()
        _pij = jnp.clip(0.00240457 * _w[:, None] * _w[None, :], 0.0, 1.0)
        _a = jax.random.uniform(jax.random.fold_in(_gk, 2), (3327, 3327)) < _pij
        _af = _a.astype(jnp.float32)
        adj = _af
        return (x, adj)
    x, adj = _rec_inputs()

    def _L0_gnn_setup():
        import jax, jax.numpy as jnp
        import numpy as np
        N = 3072
        D_IN = 256
        D_OUT = 256
        DENSITY = 0.005
        key = jax.random.key(seed)
        ks = jax.random.split(key, 12)
        x = jax.random.normal(ks[0], (N, D_IN), dtype=jnp.float32)
        adj_a = (jax.random.uniform(ks[1], (N, N)) < DENSITY).astype(jnp.float32)
        adj_b = (jax.random.uniform(ks[2], (N, N)) < DENSITY).astype(jnp.float32)
        W_sa = jax.random.normal(ks[3], (D_IN, D_OUT), dtype=jnp.float32) * (1.414 / np.sqrt(D_IN + D_OUT))
        a_sa = jax.random.normal(ks[4], (1, 2 * D_OUT), dtype=jnp.float32) * (1.414 / np.sqrt(1 + 2 * D_OUT))
        stdv = 1.0 / np.sqrt(D_OUT)
        W_gcnb = jax.random.uniform(ks[5], (D_IN, D_OUT), minval=-stdv, maxval=stdv, dtype=jnp.float32)
        b_gcnb = jax.random.uniform(ks[6], (D_OUT,), minval=-stdv, maxval=stdv, dtype=jnp.float32)
        s = 1.0 / np.sqrt(2 * D_IN)
        Wa = jax.random.uniform(ks[7], (1, 2 * D_IN), minval=-s, maxval=s, dtype=jnp.float32)
        ba = jax.random.uniform(ks[8], (1,), minval=-s, maxval=s, dtype=jnp.float32)
        Wb = jax.random.uniform(ks[9], (1, 2 * D_IN), minval=-s, maxval=s, dtype=jnp.float32)
        bb = jax.random.uniform(ks[10], (1,), minval=-s, maxval=s, dtype=jnp.float32)
        return {'x': x, 'adj_a': adj_a, 'adj_b': adj_b, 'W_sa': W_sa, 'a_sa': a_sa, 'W_gcnb': W_gcnb, 'b_gcnb': b_gcnb, 'Wa': Wa, 'ba': ba, 'Wb': Wb, 'bb': bb}
    _L0_gnn_all = _L0_gnn_setup()
    _L0_gnn_in = {k: v for k, v in _L0_gnn_all.items() if k in ('W_sa', 'a_sa', 'W_gcnb', 'b_gcnb', 'Wa', 'ba', 'Wb', 'bb')}
    del _L0_gnn_all

    def _L1_gnn_setup():
        import jax, jax.numpy as jnp
        import numpy as np
        N = 4096
        D_IN = 256
        D_OUT = 256
        NEG_BIG = -9000000000000000.0
        key = jax.random.key(seed)
        kx, ka, kw, kb, kn, ke = jax.random.split(key, 6)
        x = jax.random.normal(kx, (N, D_IN), dtype=jnp.float32)
        adj = (jax.random.uniform(ka, (N, N)) > 0.9).astype(jnp.float32)
        stdv = 1.0 / np.sqrt(D_OUT)
        weight = jax.random.uniform(kw, (D_IN, D_OUT), minval=-stdv, maxval=stdv, dtype=jnp.float32)
        bias = jax.random.uniform(kb, (D_OUT,), minval=-stdv, maxval=stdv, dtype=jnp.float32)
        node_w = jax.random.uniform(kn, (D_IN, 1), minval=-1.0, maxval=1.0, dtype=jnp.float32)
        stdv_e = 1.0 / np.sqrt(D_IN)
        edge_w = jax.random.uniform(ke, (D_IN, D_IN), minval=-stdv_e, maxval=stdv_e, dtype=jnp.float32)
        return {'x': x, 'adj': adj, 'weight': weight, 'bias': bias, 'node_w': node_w, 'edge_w': edge_w}
    _L1_gnn_all = _L1_gnn_setup()
    _L1_gnn_in = {k: v for k, v in _L1_gnn_all.items() if k in ('weight', 'bias', 'node_w', 'edge_w')}
    del _L1_gnn_all
    return {'x': x, 'adj': adj, 'L0_gnn_W_sa': _L0_gnn_in['W_sa'], 'L0_gnn_a_sa': _L0_gnn_in['a_sa'], 'L0_gnn_W_gcnb': _L0_gnn_in['W_gcnb'], 'L0_gnn_b_gcnb': _L0_gnn_in['b_gcnb'], 'L0_gnn_Wa': _L0_gnn_in['Wa'], 'L0_gnn_ba': _L0_gnn_in['ba'], 'L0_gnn_Wb': _L0_gnn_in['Wb'], 'L0_gnn_bb': _L0_gnn_in['bb'], 'L1_gnn_weight': _L1_gnn_in['weight'], 'L1_gnn_bias': _L1_gnn_in['bias'], 'L1_gnn_node_w': _L1_gnn_in['node_w'], 'L1_gnn_edge_w': _L1_gnn_in['edge_w']}

def reference(x, adj, L0_gnn_W_sa, L0_gnn_a_sa, L0_gnn_W_gcnb, L0_gnn_b_gcnb, L0_gnn_Wa, L0_gnn_ba, L0_gnn_Wb, L0_gnn_bb, L1_gnn_weight, L1_gnn_bias, L1_gnn_node_w, L1_gnn_edge_w):
    import jax
    import jax.numpy as jnp

    def _L0_gnn_ref(x, adj_a, adj_b, W_sa, a_sa, W_gcnb, b_gcnb, Wa, ba, Wb, bb):
        import jax, jax.numpy as jnp
        import numpy as np
        N = 3072
        D_IN = 256
        D_OUT = 256
        DENSITY = 0.005
        type_sum_a = adj_a @ x
        type_sum_b = adj_b @ x
        attn_a = jax.nn.sigmoid(jnp.concatenate([type_sum_a, x], axis=1) @ Wa.T + ba)
        attn_b = jax.nn.sigmoid(jnp.concatenate([type_sum_b, x], axis=1) @ Wb.T + bb)
        h = x @ W_sa
        Hd = h.shape[1]
        s_left = h @ a_sa[0, :Hd]
        s_right = h @ a_sa[0, Hd:]
        scores = s_left[:, None] + s_right[None, :]
        e = jnp.where(adj_a != 0, jnp.exp(-jax.nn.leaky_relu(scores, 0.01)), 0.0)
        attn = e / (jnp.sum(e, axis=1, keepdims=True) + 1e-05)
        x_a = attn @ h
        x_b = adj_b @ (x @ W_gcnb) + b_gcnb
        return jax.nn.sigmoid(attn_a * x_a + attn_b * x_b)

    def _L1_gnn_ref(x, adj, weight, bias, node_w, edge_w):
        import jax, jax.numpy as jnp
        import numpy as np
        N = 4096
        D_IN = 256
        D_OUT = 256
        NEG_BIG = -9000000000000000.0
        node_att = jax.nn.softmax(x @ node_w, axis=0)
        h = x @ edge_w
        e = h @ h.T
        e = jnp.where(adj > 0, e, NEG_BIG)
        edge_att = jax.nn.softmax(e, axis=1)
        combined_att = node_att * edge_att
        support = x @ weight
        output = adj * combined_att @ support
        return output + bias
    h = jnp.maximum(_layernorm(x, axis=-1), 0.0)
    x = x + _L0_gnn_ref(h, adj, adj, L0_gnn_W_sa, L0_gnn_a_sa, L0_gnn_W_gcnb, L0_gnn_b_gcnb, L0_gnn_Wa, L0_gnn_ba, L0_gnn_Wb, L0_gnn_bb)
    h = jnp.maximum(_layernorm(x, axis=-1), 0.0)
    x = x + _L1_gnn_ref(h, adj, L1_gnn_weight, L1_gnn_bias, L1_gnn_node_w, L1_gnn_edge_w)
    return x

_drawn_inputs = setup_inputs


def setup_inputs(seed=0):
    import zlib

    import numpy as np

    out = dict(_drawn_inputs(seed))
    spreads = {}
    factors = {'L0_gnn_a_sa': 8.0,
     'L0_gnn_b_gcnb': 8.0,
     'L0_gnn_Wa': 4.339,
     'L1_gnn_weight': 8.0,
     'L1_gnn_node_w': 8.0,
     'L1_gnn_edge_w': 8.0}
    for name, (base, spread) in spreads.items():
        noise = np.random.default_rng([zlib.crc32(name.encode()), seed]).standard_normal(out[name].shape)
        drawn = base * np.exp(spread * noise) if base else spread * noise
        out[name] = jnp.asarray(drawn.astype(out[name].dtype))
    for name, factor in factors.items():
        out[name] = (out[name] * factor).astype(out[name].dtype)
    return out
```

```python
from contextlib import ExitStack

import concourse.bass as bass
from concourse import mybir
from concourse.alu_op_type import AluOpType as ALU

ACT = mybir.ActivationFunctionType
F32, F16, BF16, U32 = mybir.dt.float32, mybir.dt.float16, mybir.dt.bfloat16, mybir.dt.uint32
X, XY = mybir.AxisListType.X, mybir.AxisListType.XY

P = 128
BANK = 512
H_SCALE = 16.0
W_TOP = 64.0
OUT_SCALE = 1.0 / 16.0
UNSCALE = 1.0 / (H_SCALE * W_TOP * OUT_SCALE)
G_SCALE = 1024.0
MASKED = 1.0e30
LN_EXP_SCALE = 8.317766166719343
EPS_LN, EPS_ATT = 1e-5, 1e-5

SA, GC, ED, WT, ND, SM = 0, 256, 512, 768, 1024, 1025
WCOLS = 1032
GROUPS = [(SA, 256), (GC, 256), (ED, 256), (WT, 256), (ND, 1), (SM, 6)]
G_SA, G_GC, G_ED, G_WT, G_ND, G_SM = range(6)
U_R, U_L = SM + 4, SM + 5


def build(nc, x, adj, W_sa, a_sa, W_gcnb, b_gcnb, Wa, ba, Wb, bb, weight, bias, node_w, edge_w, out):
    N, D = x.shape
    KC = D // P
    T = -(-N // P)
    NP = T * P
    TAIL = N - (T - 1) * P
    assert D == 256 and T % 2 == 0 and 0 < TAIL < P
    CHUNKS = [(c, min(BANK, NP - c)) for c in range(0, NP, BANK)]
    NCH = len(CHUNKS)
    CV = D + 2
    BPB = BANK // P
    assert NCH == 7

    with ExitStack() as ctx:
        def sb(name, shape, dt=F32):
            return ctx.enter_context(nc.sbuf_tensor(name, shape, dt))

        def sem(name):
            return ctx.enter_context(nc.semaphore(name))

        xres = sb("xres", [P, T, D])
        ident = sb("ident", [P, P])
        whi = sb("whi", [P, KC, WCOLS], F16)
        wlo = sb("wlo", [P, KC, WCOLS], F16)
        urep = sb("urep", [P, 2, KC, P], F16)
        bg = sb("bg", [P, D])
        bw = sb("bw", [P, D])
        hn = sb("hn", [P, 2, D])
        mix = sb("mix", [P, 2, D])
        act_out = sb("act_out", [P, 2, D])
        stats = sb("stats", [P, T, 6])
        mean = sb("mean", [P, T])
        var = sb("var", [P, T])
        rstd = sb("rstd", [P, T])
        tmp_t = sb("tmp_t", [P, T])
        shift = sb("shift", [P, T])
        sm = sb("sm", [P, T, 6])
        rab = sb("rab", [P, T, 2])
        eps_col = sb("eps_col", [P, T])
        srt = sb("srt", [P, T])
        gcol = sb("gcol", [P, T])
        nodes = sb("nodes", [P, T])
        amax = sb("amax", [P, 6])
        amax_all = sb("amax_all", [P, 6])
        pow2 = sb("pow2", [P, 6])
        wscale = sb("wscale", [P, 6])
        unsc = sb("unsc", [P, 6])
        cvec = sb("cvec", [P, 12])
        gates = sb("gates", [P, 2, 2])
        tg = sb("tg", [P, 2, 2])
        den = sb("den", [P, 2, 4])
        cmax = sb("cmax", [P, 2, NCH + 1])
        negm = sb("negm", [P, 2])
        bab = sb("bab", [P, 2])
        yv = sb("yv", [P, 4 * T * CV // 2])
        slb = sb("slb", [P, NP])
        adjr = sb("adjr", [P, 2, NP])
        adjt = sb("adjt", [P, 2, NP // 2])
        chain = sb("chain", [P, 2, NP])
        ehl = sb("ehl", [P, 2, NP])

        yv16 = yv[:, :].bitcast(F16)
        span = T * CV
        part = [yv16[:, q * span:(q + 1) * span].rearrange("p (t c) -> p t c", c=CV) for q in range(4)]
        y_hi, y_lo, v_hi, v_lo = part
        s_hi, s_lo = part[0], part[1]
        turned = yv16[:, 2 * span:2 * span + 2 * KC * NP].rearrange("p (q k n) -> p q k n", q=2, k=KC)
        eh_t = [turned[:, q] for q in range(2)]
        adj_t = adjt[:, :, :].bitcast(F16).rearrange("p b (t i) -> p b t i", i=P)
        maskb = adjt[:, :, :].bitcast(BF16)
        ehl16 = ehl[:, :, :].bitcast(F16)
        num = ehl16.rearrange("p b (q t i) -> p b q t i", q=2, i=P)
        rows_t = ehl16.rearrange("p q (k n) -> p q k n", k=KC)
        chain_t = chain[:, :, :].rearrange("p b (t i) -> p b t i", i=P)
        pnum = slb
        wall = chain[:, 0, 0:KC * WCOLS].rearrange("p (k c) -> p k c", k=KC)
        arow = chain[:, 1, 0:2 * D].rearrange("p (q c) -> p q c", q=2)
        scrap = chain[:, 1, 2 * D:3 * D]

        def col(n):
            return cvec[:, n:n + 1]
        srmin, nmx, nmx_all, gbias, zmax, zmax_all, zsum, zsum_all, zinv, l1scale, lnb, fac = map(col, range(12))

        tb = [ctx.enter_context(nc.psum_tensor(f"turn{k}", [P, BANK], F32)) for k in range(4)]
        acc_a = [ctx.enter_context(nc.psum_tensor(f"acc_a{b}", [P, BANK], F32)) for b in range(2)]
        acc_b = [ctx.enter_context(nc.psum_tensor(f"acc_b{b}", [P, BANK], F32)) for b in range(2)]
        sc_bank = [tb[0], tb[1], tb[2]]
        tu_bank = [tb[3], acc_a[0], acc_a[1]]

        pad_zero = sem("pad_zero")
        x_loaded = sem("x_loaded")
        w_loaded = sem("w_loaded")
        adj_ready = [sem(f"adj_ready{b}") for b in range(2)]
        adj_pad = sem("adj_pad")
        ident_ok = sem("ident_ok")
        pool_sum = sem("pool_sum")
        w_amax = sem("w_amax")
        w_split = sem("w_split")
        dve = sem("dve")
        var_ok = sem("var_ok")
        sqrt_ok = sem("sqrt_ok")
        norm_ok = sem("norm_ok")
        hn_done = sem("hn_done")
        hn_turned = sem("hn_turned")
        rows_hi = sem("rows_hi")
        rows_lo = sem("rows_lo")
        small_done = sem("small_done")
        nmx_ok = sem("nmx_ok")
        g_ok = sem("g_ok")
        gcol_ok = sem("gcol_ok")
        slb_mm = sem("slb_mm")
        slb_ok = sem("slb_ok")
        proj_mm = sem("proj_mm")
        proj_hi = sem("proj_hi")
        proj_lo = sem("proj_lo")
        turn_mm = sem("turn_mm")
        turn_out = sem("turn_out")
        sum_ok = sem("sum_ok")
        relu_ok = sem("relu_ok")
        exp_ok = sem("exp_ok")
        mask_ok = sem("mask_ok")
        num_hi = sem("num_hi")
        num_lo = sem("num_lo")
        y_done = sem("y_done")
        v_done = sem("v_done")
        gate_in = sem("gate_in")
        gate_out = sem("gate_out")
        mix_in = sem("mix_in")
        mix_out = sem("mix_out")
        fin = sem("fin")
        x1_ok = sem("x1_ok")
        st_ok = sem("st_ok")
        edge_mm = sem("edge_mm")
        edge_hi = sem("edge_hi")
        edge_lo = sem("edge_lo")
        supp_mm = sem("supp_mm")
        supp_hi = sem("supp_hi")
        supp_lo = sem("supp_lo")
        z_ok = sem("z_ok")
        zmax_in = sem("zmax_in")
        zneg_ok = sem("zneg_ok")
        zexp_ok = sem("zexp_ok")
        ones_ok = sem("ones_ok")
        mb_ok = sem("mb_ok")
        sc_mm = sem("sc_mm")
        sc_max = sem("sc_max")
        negm_ok = sem("negm_ok")
        sub_ok = sem("sub_ok")
        tu_mm = sem("tu_mm")
        p_hi = sem("p_hi")
        p_ok = sem("p_ok")
        p_lo = sem("p_lo")
        o_mm = sem("o_mm")
        fin1 = sem("fin1")
        keep_ok = sem("keep_ok")
        o_ok = sem("o_ok")
        stored = sem("stored")
        vec_mark, pool_mark = sem("vec_mark"), sem("pool_mark")

        adj_rows = adj[:, :]

        def split_product(pe, psum, parts_l, parts_r, start=True, stop=True):
            n = len(parts_l[0])
            for i, (a, c) in enumerate((a, c) for k in range(n) for a, c in
                                       ((parts_l[0][k], parts_r[0][k]), (parts_l[0][k], parts_r[1][k]),
                                        (parts_l[1][k], parts_r[0][k]))):
                mm = nc.tensor.matmul(psum, a, c, start=(i == 0), stop=(i == 3 * n - 1))
            return mm

        def carry(eng, mark):
            eng.sem_inc(mark, 1)

        def blocks(k):
            return range(k * BPB, min((k + 1) * BPB, T))

        block = ctx.enter_context(nc.Block())

        @block.sync
        def _(sp):
            body = (T - 1) * P
            half = T // 2
            sp.dma_start(xres[:, 0:half, :], x[0:half * P, :].rearrange("(t p) d -> p t d", p=P)).then_inc(x_loaded, 16)
            sp.dma_start(xres[:, half:T - 1, :], x[half * P:body, :].rearrange("(t p) d -> p t d", p=P)).then_inc(x_loaded, 16)
            sp.wait_ge(pad_zero, 1)
            sp.dma_start(xres[0:TAIL, T - 1, :], x[body:N, :]).then_inc(x_loaded, 16)

            def load(t, b, rows=P):
                sp.dma_start(adjr[0:rows, b, 0:N], adj_rows[bass.ds(t * P, rows), :]).then_inc(adj_ready[b], 16)

            load(0, 0)
            load(1, 1)
            with sp.Fori(2, T - 3, 2) as t0:
                for b in range(2):
                    sp.wait_ge(turn_mm, NCH * (t0 + b - 1))
                    load(t0 + b, b)
            sp.wait_ge(turn_mm, NCH * (T - 3))
            load(T - 2, 0)
            sp.wait_ge(turn_mm, NCH * (T - 2))
            load(T - 1, 1, TAIL)
            sp.wait_ge(turn_mm, NCH * (T - 1))
            load(0, 0)
            sp.wait_ge(turn_mm, NCH * T)
            load(1, 1)
            with sp.Fori(2, T - 3, 2) as t0:
                for b in range(2):
                    sp.wait_ge(mb_ok, t0 + b - 1)
                    load(t0 + b, b)
            sp.wait_ge(mb_ok, T - 3)
            load(T - 2, 0)
            sp.wait_ge(mb_ok, T - 2)
            load(T - 1, 1, TAIL)

        @block.gpsimd
        def _(pool):
            nc.gpsimd.memset(ident[:, :], 0.0).then_inc(ident_ok, 1)
            nc.gpsimd.memset(adjr[:, :, N:NP], 0.0).then_inc(adj_pad, 1)
            pool.wait_ge(ident_ok, 1)
            nc.gpsimd.affine_select(out=ident[:, :], in_=ident[:, :], compare_op=ALU.not_equal, fill=1.0,
                                    base=0, pattern=[[-1, P]], channel_multiplier=1).then_inc(ident_ok, 1)
            pool.wait_ge(w_amax, 1)
            nc.gpsimd.partition_all_reduce(amax_all[:, :], amax[:, :], P, bass.bass_isa.ReduceOp.max).then_inc(pool_sum, 1)
            pool.wait_ge(nmx_ok, 1)
            nc.gpsimd.partition_all_reduce(nmx_all, nmx, P, bass.bass_isa.ReduceOp.max).then_inc(pool_sum, 1)

            def low(t, b, first):
                pool.wait_ge(num_hi, t + 1)
                if not first:
                    pool.wait_ge(v_done, t - 1)
                nc.gpsimd.tensor_tensor(num[:, b, 1], chain_t[:, b], num[:, b, 0], ALU.subtract).then_inc(num_lo, 1)

            low(0, 0, True)
            low(1, 1, True)
            with pool.Fori(2, T - 1, 2) as t0:
                for b in range(2):
                    low(t0 + b, b, False)

            pool.wait_ge(z_ok, T)
            nc.gpsimd.affine_select(out=nodes[:, T - 1:T], in_=nodes[:, T - 1:T], compare_op=ALU.is_gt,
                                    fill=-MASKED, base=TAIL, pattern=[[0, 1]], channel_multiplier=-1).then_inc(pool_sum, 1)
            pool.wait_ge(zmax_in, 1)
            nc.gpsimd.partition_all_reduce(zmax_all, zmax, P, bass.bass_isa.ReduceOp.max).then_inc(pool_sum, 1)
            pool.wait_ge(zexp_ok, 1)
            nc.gpsimd.partition_all_reduce(zsum_all, zsum, P, bass.bass_isa.ReduceOp.add).then_inc(pool_sum, 1)

            def mask(t, b, first):
                if not first:
                    pool.wait_ge(sc_max, NCH * (t - 1))
                pool.wait_ge(adj_ready[b], 16 * (T // 2) + 8 * (t - b) + 16)
                carry(pool, pool_mark)
                nc.gpsimd.tensor_scalar(maskb[:, b], adjr[:, b, :], MASKED, -MASKED, ALU.mult, ALU.add).then_inc(mb_ok, 1)

            def off(t, b):
                pool.wait_ge(negm_ok, t + 1)
                carry(pool, pool_mark)
                nc.gpsimd.tensor_scalar(chain[:, b, :], chain[:, b, :], negm[:, b:b + 1], 1.0,
                                        ALU.add, ALU.mult).then_inc(sub_ok, 1)

            mask(0, 0, True)
            mask(1, 1, True)
            with pool.Fori(0, T - 3, 2) as t0:
                for b in range(2):
                    off(t0 + b, b)
                    mask(t0 + b + 2, b, False)
            off(T - 2, 0)
            off(T - 1, 1)

        @block.scalar
        def _(act):
            sa_w = [W_sa, W_gcnb, edge_w, weight]
            for n, w in enumerate(sa_w):
                act.dma_start(wall[:, :, n * D:(n + 1) * D], w.rearrange("(k p) c -> p k c", p=P)).then_inc(w_loaded, 16)
            act.dma_start(wall[:, :, ND:ND + 1], node_w.rearrange("(k p) c -> p k c", p=P),
                          allow_slow_non_contiguous=True).then_inc(w_loaded, 16)
            for q in range(2):
                for n, g in enumerate((Wa, Wb)):
                    act.dma_start(wall[:, :, SM + 2 * q + n:SM + 2 * q + n + 1],
                                  g[0:1, q * D:(q + 1) * D].rearrange("o (k p) -> p k o", p=P),
                                  allow_slow_non_contiguous=True).then_inc(w_loaded, 16)
                act.dma_start(arow[:, q, :], a_sa[0, q * D:(q + 1) * D].partition_broadcast(P)).then_inc(w_loaded, 16)
            act.dma_start(bg[:, :], b_gcnb.partition_broadcast(P)).then_inc(w_loaded, 16)
            act.dma_start(bw[:, :], bias.partition_broadcast(P)).then_inc(w_loaded, 16)
            act.dma_start(bab[:, 0:1], ba.partition_broadcast(P)).then_inc(w_loaded, 16)
            act.dma_start(bab[:, 1:2], bb.partition_broadcast(P)).then_inc(w_loaded, 16)

            def norm_and_turn(layer):
                act.wait_ge(var_ok, layer + 1)
                nc.scalar.activation(rstd[:, :], var[:, :], ACT.Sqrt).then_inc(sqrt_ok, 1)
                base = T * layer

                def norm(t, b, first):
                    if not first:
                        act.wait_ge(hn_turned, base + t - 1)
                    nc.scalar.activation(hn[:, b, :], xres[:, bass.ds(t, 1), :].squeeze(), ACT.Relu,
                                         bias=shift[:, bass.ds(t, 1)], scale=rstd[:, bass.ds(t, 1)]).then_inc(hn_done, 1)

                def high(t, b):
                    act.wait_ge(hn_turned, base + t + 1)
                    nc.scalar.activation(rows_t[:, 0, :, bass.ds(t * P, P)],
                                         tb[b][:, 0:D].rearrange("p (k n) -> p k n", k=KC), ACT.Copy).then_inc(rows_hi, 1)

                act.wait_ge(norm_ok, layer + 1)
                norm(0, 0, True)
                norm(1, 1, True)
                with act.Fori(0, T - 3, 2) as t0:
                    for b in range(2):
                        high(t0 + b, b)
                        norm(t0 + b + 2, b, False)
                high(T - 2, 0)
                high(T - 1, 1)

            norm_and_turn(0)
            act.wait_ge(g_ok, 1)
            nc.scalar.activation(gcol[:, :], sm[:, :, 4], ACT.Exp, bias=gbias, scale=-0.01).then_inc(gcol_ok, 1)
            nc.scalar.activation(eps_col[:, :], sm[:, :, 5], ACT.Exp, bias=gbias, scale=0.01).then_inc(gcol_ok, 1)

            for k, (c, w) in enumerate(CHUNKS):
                act.wait_ge(slb_mm, k + 1)
                nc.scalar.activation(slb[:, c:c + w], acc_b[k % 2][:, 0:w], ACT.Copy, scale=fac).then_inc(slb_ok, 1)

            act.wait_ge(gcol_ok, 3)

            def proj_high(t, b):
                act.wait_ge(proj_mm, t + 1)
                nc.scalar.activation(v_hi[:, bass.ds(t, 1), 0:D].squeeze(), tb[b][:, 0:D], ACT.Copy,
                                     scale=tmp_t[:, bass.ds(t, 1)]).then_inc(proj_hi, 1)
                nc.scalar.activation(y_hi[:, bass.ds(t, 1), 0:D].squeeze(), tb[b][:, D:2 * D], ACT.Copy,
                                     scale=OUT_SCALE).then_inc(proj_hi, 1)
            with act.Fori(0, T - 1, 2) as t0:
                for b in range(2):
                    proj_high(t0 + b, b)

            def gate_tanh(t, b):
                act.wait_ge(gate_in, t + 1)
                nc.scalar.activation(tg[:, b, :], gates[:, b, :], ACT.Tanh, scale=0.5).then_inc(gate_out, 1)

            def mix_tanh(t, b):
                act.wait_ge(mix_in, t + 1)
                nc.scalar.activation(act_out[:, b, :], mix[:, b, :], ACT.Tanh, scale=0.5).then_inc(mix_out, 1)

            def attend(t, b, early=False):
                if not early:
                    gate_tanh(t - 2, b)
                act.wait_ge(relu_ok, t + 1)
                nc.scalar.activation(chain[:, b, :], chain[:, b, :], ACT.Exp, scale=-0.99).then_inc(exp_ok, 1)
                for k, (c, w) in enumerate(CHUNKS):
                    act.wait_ge(turn_mm, NCH * t + k + 1)
                    if k == 0 and not early:
                        act.wait_ge(y_done, t - 1)
                        act.wait_ge(mask_ok, t - 1)
                    nc.scalar.activation(adj_t[:, b].rearrange("p t i -> p (t i)")[:, c:c + w], tb[k % 4][:, 0:w],
                                         ACT.Copy).then_inc(turn_out, 1)
                    if k == 2 and not early:
                        mix_tanh(t - 2, b)
                act.wait_ge(mask_ok, t + 1)
                if not early:
                    act.wait_ge(v_done, t - 1)
                nc.scalar.activation(num[:, b, 0], chain_t[:, b], ACT.Copy).then_inc(num_hi, 1)

            attend(0, 0, True)
            attend(1, 1, True)
            with act.Fori(2, T - 1, 2) as t0:
                for b in range(2):
                    attend(t0 + b, b)
            for t in (T - 2, T - 1):
                gate_tanh(t, t % 2)
                mix_tanh(t, t % 2)

            norm_and_turn(1)

            def edge_high(k, c, w):
                for m in range(KC):
                    act.wait_ge(edge_mm, KC * k + m + 1)
                    nc.scalar.activation(eh_t[0][:, m, bass.ds(c, w)], acc_a[m][:, 0:w], ACT.Copy,
                                         scale=OUT_SCALE).then_inc(edge_hi, 1)
            with act.Fori(0, NCH - 1) as k:
                edge_high(k, k * BANK, BANK)
            edge_high(NCH - 1, *CHUNKS[-1])

            def supp_high(t, b):
                act.wait_ge(supp_mm, t + 1)
                nc.scalar.activation(s_hi[:, bass.ds(t, 1), 0:D].squeeze(), acc_b[b][:, 0:D], ACT.Copy,
                                     scale=OUT_SCALE).then_inc(supp_hi, 1)
            with act.Fori(0, T - 1, 2) as t0:
                for b in range(2):
                    supp_high(t0 + b, b)
            act.wait_ge(zneg_ok, 1)
            nc.scalar.activation(nodes[:, :], nodes[:, :], ACT.Exp, bias=zmax_all, accum_out=zsum).then_inc(zexp_ok, 1)

            def numer(t, b, first):
                for k, (c, w) in enumerate(CHUNKS):
                    act.wait_ge(tu_mm, NCH * t + k + 1)
                    if k == 0 and not first:
                        act.wait_ge(o_mm, t - 1)
                    nc.scalar.activation(num[:, b, 0].rearrange("p t i -> p (t i)")[:, c:c + w], tu_bank[k % 3][:, 0:w],
                                         ACT.Exp, bias=lnb, scale=l1scale).then_inc(p_hi, 1)
                    if not (first and t == 0):
                        act.wait_ge(p_lo, NCH * (t - 1) + k + 1)
                    nc.scalar.activation(pnum[:, c:c + w], tu_bank[k % 3][:, 0:w], ACT.Exp, bias=lnb,
                                         scale=l1scale).then_inc(p_ok, 1)

            numer(0, 0, True)
            numer(1, 1, True)
            with act.Fori(2, T - 1, 2) as t0:
                for b in range(2):
                    numer(t0 + b, b, False)
                    act.wait_ge(o_ok, t0 + b - 1)
                    act.dma_start(out[bass.ds((t0 + b - 2) * P, P), :],
                                  xres[:, bass.ds(t0 + b - 2, 1), :].squeeze()).then_inc(stored, 16)
            act.wait_ge(o_ok, T - 1)
            act.dma_start(out[(T - 2) * P:(T - 1) * P, :], xres[:, T - 2, :]).then_inc(stored, 16)
            act.wait_ge(o_ok, T)
            act.dma_start(out[(T - 1) * P:N, :], xres[0:TAIL, T - 1, :]).then_inc(stored, 16)
            act.wait_ge(stored, 16 * T)

        @block.vector
        def _(vec):
            count = [0]

            def step(ins):
                count[0] += 1
                ins.then_inc(dve, 1)
                vec.wait_ge(dve, count[0])

            v = nc.vector
            v.memset(xres[96:P, T - 1, :], 0.0).then_inc(pad_zero, 1)
            step(v.memset(lnb, LN_EXP_SCALE))
            step(v.memset(wall[:, :, WCOLS - 1:WCOLS], 0.0))
            vec.wait_ge(w_loaded, 16 * 15)
            for k in range(KC):
                for q, c in ((1, U_R), (0, U_L)):
                    step(v.tensor_tensor_reduce(out=scrap, in0=wall[:, k, SA:SA + D], in1=arow[:, q, :], scale=1.0,
                                                scalar=0.0, op0=ALU.mult, op1=ALU.add, accum_out=wall[:, k, c:c + 1]))
            for g, (c, w) in enumerate(GROUPS):
                step(v.tensor_reduce(amax[:, g:g + 1], wall[:, :, c:c + w], XY, ALU.max, apply_absolute_value=True))
            step(v.tensor_scalar(amax[:, :], amax[:, :], 1e-30, None, ALU.max))
            v.nop().then_inc(w_amax, 1)
            vec.wait_ge(pool_sum, 1)
            step(v.tensor_scalar(pow2[:, :].bitcast(U32), amax_all[:, :].bitcast(U32), 0x7F800000, None, ALU.bitwise_and))
            step(v.reciprocal(wscale[:, :], pow2[:, :]))
            step(v.tensor_scalar(wscale[:, :], wscale[:, :], W_TOP, None, ALU.mult))
            step(v.tensor_scalar(unsc[:, :], pow2[:, :], UNSCALE, None, ALU.mult))
            for g, (c, w) in enumerate(GROUPS):
                step(v.tensor_scalar(wall[:, :, c:c + w], wall[:, :, c:c + w], wscale[:, g:g + 1], None, ALU.mult))
            step(v.tensor_copy(whi[:, :, :], wall[:, :, :]))
            step(v.tensor_tensor(wlo[:, :, :], wall[:, :, :], whi[:, :, :], ALU.subtract))
            for q, part16 in enumerate((whi, wlo)):
                step(v.tensor_copy(urep[:, q], part16[:, :, U_L:U_L + 1].broadcast_to([P, KC, P])))
            step(v.tensor_tensor(l1scale, unsc[:, G_ED:G_ED + 1], unsc[:, G_ED:G_ED + 1], ALU.mult))
            v.nop().then_inc(w_split, 1)

            def norm_stats(layer):
                step(v.tensor_tensor(mean[:, :], stats[:, :, 1], stats[:, :, 4], ALU.add))
                step(v.tensor_tensor(tmp_t[:, :], stats[:, :, 1], stats[:, :, 4], ALU.subtract))
                step(v.tensor_scalar(mean[:, :], mean[:, :], 0.5, None, ALU.mult))
                step(v.tensor_tensor(tmp_t[:, :], tmp_t[:, :], tmp_t[:, :], ALU.mult))
                step(v.tensor_tensor(var[:, :], stats[:, :, 2], stats[:, :, 5], ALU.add))
                step(v.tensor_scalar(tmp_t[:, :], tmp_t[:, :], 0.25, EPS_LN, ALU.mult, ALU.add))
                step(v.scalar_tensor_tensor(out=var[:, :], in0=var[:, :], scalar=1.0 / D, in1=tmp_t[:, :],
                                            op0=ALU.mult, op1=ALU.add))
                v.nop().then_inc(var_ok, 1)
                vec.wait_ge(sqrt_ok, layer + 1)
                step(v.reciprocal(rstd[:, :], rstd[:, :]))
                step(v.tensor_tensor(tmp_t[:, :], rstd[:, :], rstd[:, :], ALU.mult))
                step(v.tensor_tensor(tmp_t[:, :], tmp_t[:, :], var[:, :], ALU.mult))
                step(v.tensor_scalar(tmp_t[:, :], tmp_t[:, :], -0.5 * H_SCALE, 1.5 * H_SCALE, ALU.mult, ALU.add))
                step(v.tensor_tensor(rstd[:, :], rstd[:, :], tmp_t[:, :], ALU.mult))
                step(v.scalar_tensor_tensor(out=shift[:, :], in0=mean[:, :], scalar=-1.0, in1=rstd[:, :],
                                            op0=ALU.mult, op1=ALU.mult))
                v.nop().then_inc(norm_ok, 1)

            def rows_low(layer):
                with vec.Fori(0, T - 1, 2) as t0:
                    for b in range(2):
                        t = t0 + b
                        vec.wait_ge(rows_hi, T * layer + t + 1)
                        v.tensor_tensor(rows_t[:, 1, :, bass.ds(t * P, P)], tb[b][:, 0:D].rearrange("p (k n) -> p k n", k=KC),
                                        rows_t[:, 0, :, bass.ds(t * P, P)], ALU.subtract).then_inc(rows_lo, 1)

            vec.wait_ge(x_loaded, 48)
            with vec.Fori(0, T) as t:
                v.bn_stats(stats[:, bass.ds(t, 1), :].squeeze(), xres[:, bass.ds(t, 1), :].squeeze()).then_inc(st_ok, 1)
            vec.wait_ge(st_ok, T)
            norm_stats(0)
            rows_low(0)

            vec.wait_ge(small_done, T)
            small = acc_a[0][:, 0:8 * T].rearrange("p (t c) -> p t c", c=8)
            v.tensor_scalar(fac, unsc[:, G_SM:G_SM + 1], OUT_SCALE, None, ALU.mult).then_inc(dve, 1)
            count[0] += 1
            vec.wait_ge(dve, count[0])
            step(v.tensor_scalar(sm[:, :, :], small[:, :, 0:6], fac, None, ALU.mult))
            for n in range(2):
                step(v.tensor_scalar(rab[:, :, n], sm[:, :, 2 + n], bab[:, n:n + 1], None, ALU.add))
            step(v.tensor_reduce(srmin, sm[:, :, 4], X, ALU.min))
            step(v.tensor_scalar(nmx, srmin, -1.0, None, ALU.mult))
            v.nop().then_inc(nmx_ok, 1)
            step(v.tensor_scalar(sm[:, :, 2:4], small[:, :, 0:2], OUT_SCALE, None, ALU.mult))
            step(v.tensor_copy(y_hi[:, :, D:D + 2], sm[:, :, 2:4]))
            step(v.tensor_tensor(y_lo[:, :, D:D + 2], sm[:, :, 2:4], y_hi[:, :, D:D + 2], ALU.subtract))
            vec.wait_ge(pool_sum, 2)
            step(v.tensor_scalar(gbias, nmx_all, -0.01, None, ALU.mult))
            v.nop().then_inc(g_ok, 1)
            vec.wait_ge(gcol_ok, 2)
            step(v.tensor_scalar(eps_col[:, :], eps_col[:, :], EPS_ATT * G_SCALE, None, ALU.mult))
            step(v.tensor_scalar(tmp_t[:, :], gcol[:, :], G_SCALE, None, ALU.mult))
            step(v.tensor_copy(v_hi[:, :, D], tmp_t[:, :]))
            step(v.tensor_tensor(v_lo[:, :, D], tmp_t[:, :], v_hi[:, :, D], ALU.subtract))
            step(v.tensor_scalar(tmp_t[:, :], gcol[:, :], OUT_SCALE, None, ALU.mult))
            v.nop().then_inc(gcol_ok, 1)
            step(v.tensor_copy(srt[:, :], sm[:, :, 4]))

            with vec.Fori(0, T - 1, 2) as t0:
                for b in range(2):
                    t = t0 + b
                    vec.wait_ge(proj_hi, 2 * t + 2)
                    v.scalar_tensor_tensor(out=v_lo[:, bass.ds(t, 1), 0:D].squeeze(), in0=tb[b][:, 0:D],
                                           scalar=tmp_t[:, bass.ds(t, 1)], in1=v_hi[:, bass.ds(t, 1), 0:D].squeeze(),
                                           op0=ALU.mult, op1=ALU.subtract).then_inc(proj_lo, 1)
                    v.scalar_tensor_tensor(out=y_lo[:, bass.ds(t, 1), 0:D].squeeze(), in0=tb[b][:, D:2 * D],
                                           scalar=OUT_SCALE, in1=y_hi[:, bass.ds(t, 1), 0:D].squeeze(),
                                           op0=ALU.mult, op1=ALU.subtract).then_inc(proj_lo, 1)
            vec.wait_ge(slb_ok, NCH)
            step(v.tensor_scalar(fac, unsc[:, G_SA:G_SA + 1], G_SCALE, None, ALU.mult))

            FIN = 9

            def finish_a(t, b):
                vec.wait_ge(v_done, t + 1)
                v.scalar_tensor_tensor(out=gates[:, b, :], in0=acc_a[b][:, D:D + 2], scalar=unsc[:, G_SM:G_SM + 1],
                                       in1=rab[:, bass.ds(t, 1), :].squeeze(), op0=ALU.mult, op1=ALU.add).then_inc(gate_in, 1)
                v.tensor_scalar(den[:, b, 0:1], acc_b[b][:, D:D + 1], eps_col[:, bass.ds(t, 1)], None,
                                ALU.add).then_inc(fin, 1)
                v.scalar_tensor_tensor(out=mix[:, b, :], in0=acc_a[b][:, 0:D], scalar=unsc[:, G_GC:G_GC + 1],
                                       in1=bg[:, :], op0=ALU.mult, op1=ALU.add).then_inc(fin, 1)
                vec.wait_ge(fin, FIN * t + 1)
                v.reciprocal(den[:, b, 1:2], den[:, b, 0:1]).then_inc(fin, 1)

            def finish_b(t, b):
                vec.wait_ge(gate_out, t + 1)
                v.tensor_scalar(tg[:, b, :], tg[:, b, :], 0.5, 0.5, ALU.mult, ALU.add).then_inc(fin, 1)
                vec.wait_ge(fin, FIN * t + 4)
                v.tensor_scalar(den[:, b, 2:3], tg[:, b, 0:1], den[:, b, 1:2], fac, ALU.mult, ALU.mult).then_inc(fin, 1)
                v.tensor_scalar(mix[:, b, :], mix[:, b, :], tg[:, b, 1:2], None, ALU.mult).then_inc(fin, 1)
                vec.wait_ge(fin, FIN * t + 6)
                v.scalar_tensor_tensor(out=mix[:, b, :], in0=acc_b[b][:, 0:D], scalar=den[:, b, 2:3],
                                       in1=mix[:, b, :], op0=ALU.mult, op1=ALU.add).then_inc(mix_in, 1)

            def finish_c(t, b):
                vec.wait_ge(mix_out, t + 1)
                v.tensor_scalar(act_out[:, b, :], act_out[:, b, :], 0.5, 0.5, ALU.mult, ALU.add).then_inc(fin, 1)
                vec.wait_ge(fin, FIN * t + 7)
                xt = xres[:, bass.ds(t, 1), :].squeeze()
                v.tensor_tensor(xt, act_out[:, b, :], xt, ALU.add).then_inc(fin, 1)
                vec.wait_ge(fin, FIN * t + 8)
                v.bn_stats(stats[:, bass.ds(t, 1), :].squeeze(), xt).then_inc(fin, 1)

            def attend(t, b, early=False):
                if not early:
                    vec.wait_ge(num_lo, t - 1)
                v.tensor_tensor(chain_t[:, b], slb[:, bass.ds(t * P, P)].unsqueeze(1).broadcast_to([P, T, P]),
                                srt[:, :].unsqueeze(2).broadcast_to([P, T, P]), ALU.add).then_inc(sum_ok, 1)
                vec.wait_ge(sum_ok, t + 1)
                v.tensor_scalar(chain[:, b, :], chain[:, b, :], 0.0, None, ALU.max).then_inc(relu_ok, 1)
                if not early:
                    finish_a(t - 2, b)
                    finish_b(t - 2, b)
                    finish_c(t - 2, b)
                vec.wait_ge(exp_ok, t + 1)
                vec.wait_ge(turn_out, NCH * (t + 1))
                v.tensor_tensor(chain_t[:, b], chain_t[:, b], adj_t[:, b], ALU.mult).then_inc(mask_ok, 1)

            attend(0, 0, True)
            attend(1, 1, True)
            with vec.Fori(2, T - 1, 2) as t0:
                for b in range(2):
                    attend(t0 + b, b)
            for t in (T - 2, T - 1):
                finish_a(t, t % 2)
                finish_b(t, t % 2)
                finish_c(t, t % 2)

            vec.wait_ge(fin, FIN * T)
            norm_stats(1)
            rows_low(1)

            def edge_low(k, c, w):
                for m in range(KC):
                    vec.wait_ge(edge_hi, KC * k + m + 1)
                    v.scalar_tensor_tensor(out=eh_t[1][:, m, bass.ds(c, w)], in0=acc_a[m][:, 0:w], scalar=OUT_SCALE,
                                           in1=eh_t[0][:, m, bass.ds(c, w)], op0=ALU.mult,
                                           op1=ALU.subtract).then_inc(edge_lo, 1)
            with vec.Fori(0, NCH - 1) as k:
                edge_low(k, k * BANK, BANK)
            edge_low(NCH - 1, *CHUNKS[-1])
            step(v.tensor_scalar(fac, unsc[:, G_ND:G_ND + 1], OUT_SCALE, None, ALU.mult))
            with vec.Fori(0, T - 1, 2) as t0:
                for b in range(2):
                    t = t0 + b
                    vec.wait_ge(supp_hi, t + 1)
                    v.tensor_scalar(nodes[:, bass.ds(t, 1)], acc_b[b][:, D:D + 1], fac, None, ALU.mult).then_inc(z_ok, 1)
                    v.scalar_tensor_tensor(out=s_lo[:, bass.ds(t, 1), 0:D].squeeze(), in0=acc_b[b][:, 0:D],
                                           scalar=OUT_SCALE, in1=s_hi[:, bass.ds(t, 1), 0:D].squeeze(),
                                           op0=ALU.mult, op1=ALU.subtract).then_inc(supp_lo, 1)
            step(v.memset(s_hi[:, :, D:CV], 1.0))
            step(v.memset(s_lo[:, :, D:CV], 0.0))
            v.nop().then_inc(ones_ok, 1)
            vec.wait_ge(pool_sum, 3)
            step(v.tensor_reduce(zmax, nodes[:, :], X, ALU.max))
            v.nop().then_inc(zmax_in, 1)
            vec.wait_ge(pool_sum, 4)
            step(v.tensor_scalar(zmax_all, zmax_all, -1.0, None, ALU.mult))
            v.nop().then_inc(zneg_ok, 1)
            vec.wait_ge(pool_sum, 5)
            step(v.reciprocal(zinv, zsum_all))
            step(v.tensor_scalar(nodes[:, :], nodes[:, :], zinv, unsc[:, G_WT:G_WT + 1], ALU.mult, ALU.mult))

            F1 = 3

            def scan(t, b, k, c, w, first):
                if k == 0:
                    vec.wait_ge(mb_ok, t + 1)
                    if not first:
                        vec.wait_ge(tu_mm, NCH * (t - 1))
                vec.wait_ge(sc_mm, NCH * t + k + 1)
                carry(vec, vec_mark)
                v.tensor_tensor_reduce(out=chain[:, b, c:c + w], in0=sc_bank[k % 3][:, 0:w], in1=maskb[:, b, c:c + w],
                                       scale=1.0, scalar=-3.0e38, op0=ALU.add, op1=ALU.max,
                                       accum_out=cmax[:, b, k:k + 1]).then_inc(sc_max, 1)

            def top(t, b):
                vec.wait_ge(sc_max, NCH * (t + 1))
                v.tensor_reduce(negm[:, b:b + 1], cmax[:, b, 0:NCH], X, ALU.max, negate=True).then_inc(negm_ok, 1)

            def low(t, b, k, c, w):
                vec.wait_ge(p_ok, NCH * t + k + 1)
                if k == 0:
                    pass
                v.tensor_tensor(num[:, b, 1].rearrange("p t i -> p (t i)")[:, c:c + w], pnum[:, c:c + w],
                                num[:, b, 0].rearrange("p t i -> p (t i)")[:, c:c + w], ALU.subtract).then_inc(p_lo, 1)

            def keep(t, b):
                vec.wait_ge(negm_ok, t + 1)
                v.tensor_scalar(den[:, b, 3:4], negm[:, b:b + 1], 0.5 * MASKED, None, ALU.is_lt).then_inc(keep_ok, 1)

            def finish(t, b):
                vec.wait_ge(o_mm, t + 1)
                v.reciprocal(den[:, b, 0:1], acc_b[b][:, D:D + 1]).then_inc(fin1, 1)
                vec.wait_ge(fin1, F1 * t + 1)
                vec.wait_ge(keep_ok, t + 1)
                v.tensor_scalar(den[:, b, 1:2], den[:, b, 0:1], nodes[:, bass.ds(t, 1)], den[:, b, 3:4],
                                ALU.mult, ALU.mult).then_inc(fin1, 1)
                vec.wait_ge(fin1, F1 * t + 2)
                xt = xres[:, bass.ds(t, 1), :].squeeze()
                v.scalar_tensor_tensor(out=mix[:, b, :], in0=acc_b[b][:, 0:D], scalar=den[:, b, 1:2], in1=xt,
                                       op0=ALU.mult, op1=ALU.add).then_inc(fin1, 1)
                vec.wait_ge(fin1, F1 * t + 3)
                v.tensor_tensor(xt, mix[:, b, :], bw[:, :], ALU.add).then_inc(o_ok, 1)

            def tile(t, b, first=False, last=False, before=True):
                keep(t, b)
                for k, (c, w) in enumerate(CHUNKS):
                    if not last:
                        scan(t + 1, 1 - b, k, c, w, first)
                    low(t, b, k, c, w)
                    if k == 2 and before:
                        finish(t - 1, 1 - b)
                if not last:
                    top(t + 1, 1 - b)

            for k, (c, w) in enumerate(CHUNKS):
                scan(0, 0, k, c, w, True)
            top(0, 0)
            vec.wait_ge(negm_ok, 1)
            tile(0, 0, first=True, before=False)
            tile(1, 1)
            with vec.Fori(2, T - 3, 2) as t0:
                for b in range(2):
                    tile(t0 + b, b)
            tile(T - 2, 0)
            tile(T - 1, 1, last=True)
            finish(T - 1, 1)

        @block.tensor
        def _(pe):
            pe.wait_ge(ident_ok, 2)

            def rows_turned(layer):
                base = T * layer
                def turn(t, b, first):
                    pe.wait_ge(hn_done, base + t + 1)
                    if not first:
                        pe.wait_ge(rows_lo, base + t - 1)
                    for k in range(KC):
                        tr = nc.tensor.transpose(tb[b][:, k * P:(k + 1) * P], hn[:, b, k * P:(k + 1) * P], ident[:, :])
                    tr.then_inc(hn_turned, 1)
                turn(0, 0, True)
                turn(1, 1, True)
                with pe.Fori(2, T - 1, 2) as t0:
                    for b in range(2):
                        turn(t0 + b, b, False)
                pe.wait_ge(rows_lo, base + T)

            def lhs(t):
                return [[rows_t[:, q, k, bass.ds(t * P, P)] for k in range(KC)] for q in range(2)]

            def wcols(c, w):
                return [[m[:, k, c:c + w] for k in range(KC)] for m in (whi, wlo)]

            rows_turned(0)
            pe.wait_ge(w_split, 1)
            with pe.Fori(0, T) as t:
                split_product(pe, acc_a[0][:, bass.ds(t * 8, 6)], lhs(t), wcols(SM, 6)).then_inc(small_done, 1)
            for k, (c, w) in enumerate(CHUNKS):
                if k >= 2:
                    pe.wait_ge(slb_ok, k - 1)
                split_product(pe, acc_b[k % 2][:, 0:w], [[urep[:, q, m] for m in range(KC)] for q in range(2)],
                              [[rows_t[:, q, m, c:c + w] for m in range(KC)] for q in range(2)]).then_inc(slb_mm, 1)

            def project(t, b, first):
                if not first:
                    pe.wait_ge(proj_lo, 2 * t - 2)
                split_product(pe, tb[b][:, :], lhs(t), wcols(SA, 2 * D)).then_inc(proj_mm, 1)
            project(0, 0, True)
            project(1, 1, True)
            with pe.Fori(2, T - 1, 2) as t0:
                for b in range(2):
                    project(t0 + b, b, False)
            pe.wait_ge(proj_lo, 2 * T)

            def turn(t, b, k, first=False, third=None):
                if k == 0:
                    pe.wait_ge(adj_ready[b], 8 * (t - b) + 16)
                if k >= 4:
                    pe.wait_ge(turn_out, NCH * t + k - 3)
                elif not first:
                    pe.wait_ge(turn_out, NCH * t + k - 2 if k < 3 else NCH * t - 3)
                for j, m in enumerate(blocks(k)):
                    tr = nc.tensor.transpose(tb[k % 4][:, j * P:(j + 1) * P], adjr[:, b, m * P:(m + 1) * P], ident[:, :])
                tr.then_inc(turn_mm, 1)

            def attend(t, b, early=False, last=False):
                if not early:
                    pe.wait_ge(mix_in, t - 1)
                for k in range(NCH):
                    if not last:
                        turn(t + 1, 1 - b, k)
                    pe.wait_ge(turn_out, NCH * t + k + 1)
                    for m in blocks(k):
                        for q, y in enumerate((y_hi, y_lo)):
                            mm = nc.tensor.matmul(acc_a[b][:, 0:CV], adj_t[:, b, m], y[:, m, :],
                                                  start=(m == 0 and q == 0), stop=(m == T - 1 and q == 1))
                mm.then_inc(y_done, 1)
                pe.wait_ge(num_hi, t + 1)
                for m in range(T):
                    for q, y in enumerate((v_hi, v_lo)):
                        nc.tensor.matmul(acc_b[b][:, 0:D + 1], num[:, b, 0, m], y[:, m, 0:D + 1],
                                         start=(m == 0 and q == 0), stop=False)
                pe.wait_ge(num_lo, t + 1)
                for m in range(T):
                    mm = nc.tensor.matmul(acc_b[b][:, 0:D + 1], num[:, b, 1, m], v_hi[:, m, 0:D + 1],
                                          start=False, stop=(m == T - 1))
                mm.then_inc(v_done, 1)

            pe.wait_ge(adj_pad, 1)
            for k in range(NCH):
                turn(0, 0, k, first=True)
            attend(0, 0, early=True)
            attend(1, 1, early=True)
            with pe.Fori(2, T - 3, 2) as t0:
                for b in range(2):
                    attend(t0 + b, b)
            attend(T - 2, 0)
            attend(T - 1, 1, last=True)

            pe.wait_ge(mix_in, T)
            rows_turned(1)

            def edge(k, c, w, first=False):
                for m in range(KC):
                    if not first:
                        pe.wait_ge(edge_lo, KC * (k - 1) + m + 1)
                    split_product(pe, acc_a[m][:, 0:w], wcols_edge(m), [[rows_t[:, q, j, bass.ds(c, w)] for j in range(KC)]
                                                                        for q in range(2)]).then_inc(edge_mm, 1)

            def wcols_edge(m):
                return wcols(ED + m * P, P)
            edge(0, 0, BANK, first=True)
            with pe.Fori(1, NCH - 1) as k:
                edge(k, k * BANK, BANK)
            edge(NCH - 1, *CHUNKS[-1])

            def support(t, b, first):
                if not first:
                    pe.wait_ge(supp_lo, t - 1)
                split_product(pe, acc_b[b][:, 0:D + 1], lhs(t), wcols(WT, D + 1)).then_inc(supp_mm, 1)
            support(0, 0, True)
            support(1, 1, True)
            with pe.Fori(2, T - 1, 2) as t0:
                for b in range(2):
                    support(t0 + b, b, False)
            pe.wait_ge(supp_lo, T)
            pe.wait_ge(ones_ok, 1)

            def score(t, k, c, w, first=False):
                if not (first and k < 3):
                    prev = {0: 6, 1: 4, 2: 5}[k] + 1 - NCH if k < 3 else k - 2
                    pe.wait_ge(sc_max, NCH * t + prev)
                split_product(pe, sc_bank[k % 3][:, 0:w], [[eh_t[q][:, j, bass.ds(t * P, P)] for j in range(KC)] for q in range(2)],
                              [[eh_t[q][:, j, c:c + w] for j in range(KC)] for q in range(2)]).then_inc(sc_mm, 1)

            def turn_scores(t, b, k, first=False):
                if k == 0:
                    pe.wait_ge(sub_ok, t + 1)
                if not (first and k < 3):
                    prev = {0: 6, 1: 4, 2: 5}[k] + 1 - NCH if k < 3 else k - 2
                    pe.wait_ge(p_ok, NCH * t + prev)
                for j, m in enumerate(blocks(k)):
                    tr = nc.tensor.transpose(tu_bank[k % 3][:, j * P:(j + 1) * P], chain_t[:, b, m], ident[:, :])
                tr.then_inc(tu_mm, 1)

            def rows_out(t, b, first=False):
                if not first:
                    pe.wait_ge(fin1, F1 * (t - 1))
                for k in range(NCH):
                    pe.wait_ge(p_lo, NCH * t + k + 1)
                    for m in blocks(k):
                        for a, s in ((0, s_hi), (0, s_lo), (1, s_hi)):
                            mm = nc.tensor.matmul(acc_b[b][:, 0:D + 1], num[:, b, a, m], s[:, m, 0:D + 1],
                                                  start=(m == 0 and a == 0 and s is s_hi), stop=(m == T - 1 and a == 1))
                mm.then_inc(o_mm, 1)

            def tile(t, b, first=False, last=False, early=False):
                for k, (c, w) in enumerate(CHUNKS):
                    if not last:
                        score(t + 1, k, c, w)
                    turn_scores(t, b, k, first)
                rows_out(t, b, early)

            F1 = 3
            for k, (c, w) in enumerate(CHUNKS):
                score(0, k, c, w, True)
            tile(0, 0, first=True, early=True)
            tile(1, 1, early=True)
            with pe.Fori(2, T - 3, 2) as t0:
                for b in range(2):
                    tile(t0 + b, b)
            tile(T - 2, 0)
            tile(T - 1, 1, last=True)


_INS = ['x', 'adj', 'L0_gnn_W_sa', 'L0_gnn_a_sa', 'L0_gnn_W_gcnb', 'L0_gnn_b_gcnb', 'L0_gnn_Wa', 'L0_gnn_ba',
        'L0_gnn_Wb', 'L0_gnn_bb', 'L1_gnn_weight', 'L1_gnn_bias', 'L1_gnn_node_w', 'L1_gnn_edge_w']


def kernel(**inputs):
    import numpy as _np
    import concourse.bacc as _bacc
    from concourse import mybir as _mybir
    from concourse.bass_utils import run_bass_kernel_spmd as _run

    nc = _bacc.Bacc("TRN2", target_bir_lowering=False, num_devices=1)
    arrays, args = {}, []
    for name in _INS:
        a = _np.ascontiguousarray(inputs[name])
        arrays[f"in_{name}"] = a
        args.append(nc.dram_tensor(f"in_{name}", a.shape, _mybir.dt.from_np(a.dtype), kind="ExternalInput").ap())
    out = nc.dram_tensor("out_x", inputs['x'].shape, _mybir.dt.float32, kind="ExternalOutput").ap()
    build(nc, *args, out)
    r = _run(nc, [arrays], core_ids=[0])
    return r.results[0]["out_x"]
```

```python
from contextlib import ExitStack

import concourse.bass as bass
from concourse import mybir
from concourse.alu_op_type import AluOpType as ALU

ACT = mybir.ActivationFunctionType
F32, F16, BF16, U32 = mybir.dt.float32, mybir.dt.float16, mybir.dt.bfloat16, mybir.dt.uint32
X, XY = mybir.AxisListType.X, mybir.AxisListType.XY

P = 128
BANK = 512
H_SCALE = 16.0
W_TOP = 64.0
OUT_SCALE = 1.0 / 16.0
UNSCALE = 1.0 / (H_SCALE * W_TOP * OUT_SCALE)
G_SCALE = 1024.0
MASKED = 1.0e30
LN_EXP_SCALE = 8.317766166719343
EPS_LN, EPS_ATT = 1e-5, 1e-5

SA, GC, ED, WT, ND, SM = 0, 256, 512, 768, 1024, 1025
WCOLS = 1032
GROUPS = [(SA, 256), (GC, 256), (ED, 256), (WT, 256), (ND, 1), (SM, 6)]
G_SA, G_GC, G_ED, G_WT, G_ND, G_SM = range(6)
U_R, U_L = SM + 4, SM + 5


def build(nc, x, adj, W_sa, a_sa, W_gcnb, b_gcnb, Wa, ba, Wb, bb, weight, bias, node_w, edge_w, out):
    N, D = x.shape
    KC = D // P
    T = -(-N // P)
    NP = T * P
    TAIL = N - (T - 1) * P
    assert D == 256 and T % 2 == 0 and 0 < TAIL < P
    CHUNKS = [(c, min(BANK, NP - c)) for c in range(0, NP, BANK)]
    NCH = len(CHUNKS)
    CV = D + 2
    BPB = BANK // P
    GROUPS_T = [(g, min(2 * BPB, T - g)) for g in range(0, T, 2 * BPB)]
    NG = len(GROUPS_T)
    assert NG == 4
    assert NCH == 7

    with ExitStack() as ctx:
        def sb(name, shape, dt=F32):
            return ctx.enter_context(nc.sbuf_tensor(name, shape, dt))

        def sem(name):
            return ctx.enter_context(nc.semaphore(name))

        xres = sb("xres", [P, T, D])
        ident = sb("ident", [P, P])
        ident16 = sb("ident16", [P, P], F16)
        whi = sb("whi", [P, KC, WCOLS], F16)
        wlo = sb("wlo", [P, KC, WCOLS], F16)
        urep = sb("urep", [P, 2, KC, P], F16)
        bg = sb("bg", [P, D])
        bw = sb("bw", [P, D])
        mix = sb("mix", [P, 2, D])
        act_out = sb("act_out", [P, 2, D])
        hn = act_out
        stats = sb("stats", [P, T, 6])
        mean = sb("mean", [P, T])
        var = sb("var", [P, T])
        rstd = sb("rstd", [P, T])
        tmp_t = sb("tmp_t", [P, T])
        shift = sb("shift", [P, T])
        sm = sb("sm", [P, T, 6])
        rab = sb("rab", [P, T, 2])
        eps_col = sb("eps_col", [P, T])
        srt = sb("srt", [P, T])
        gcol = sb("gcol", [P, T])
        nodes = sb("nodes", [P, T])
        amax = sb("amax", [P, 6])
        amax_all = sb("amax_all", [P, 6])
        pow2 = sb("pow2", [P, 6])
        wscale = sb("wscale", [P, 6])
        unsc = sb("unsc", [P, 6])
        cvec = sb("cvec", [P, 12])
        gates = sb("gates", [P, 2, 2])
        tg = sb("tg", [P, 2, 2])
        den = sb("den", [P, 2, 4])
        cmax = sb("cmax", [P, 2, NCH + 1])
        negm = sb("negm", [P, 2])
        bab = sb("bab", [P, 2])
        yv = sb("yv", [P, 4 * T * CV // 2])
        slb = sb("slb", [P, NP])
        adjr = sb("adjr", [P, 2, NP])
        adj16 = sb("adj16", [P, NP], F16)
        adjt = sb("adjt", [P, 2, NP // 2])
        chain = sb("chain", [P, 2, NP])
        ehl = sb("ehl", [P, 2, NP])

        yv16 = yv[:, :].bitcast(F16)
        span = T * CV
        part = [yv16[:, q * span:(q + 1) * span].rearrange("p (t c) -> p t c", c=CV) for q in range(4)]
        y_hi, y_lo, v_hi, v_lo = part
        s_hi, s_lo = part[0], part[1]
        turned = yv16[:, 2 * span:2 * span + 2 * KC * NP].rearrange("p (q k n) -> p q k n", q=2, k=KC)
        eh_t = [turned[:, q] for q in range(2)]
        adj_t = adjt[:, :, :].bitcast(F16).rearrange("p b (t i) -> p b t i", i=P)
        maskb = adjt[:, :, :].bitcast(BF16)
        ehl16 = ehl[:, :, :].bitcast(F16)
        num = ehl16.rearrange("p b (q t i) -> p b q t i", q=2, i=P)
        rows_t = ehl16.rearrange("p q (k n) -> p q k n", k=KC)
        chain_t = chain[:, :, :].rearrange("p b (t i) -> p b t i", i=P)
        pnum = slb
        wall = chain[:, 0, 0:KC * WCOLS].rearrange("p (k c) -> p k c", k=KC)
        arow = chain[:, 1, 0:2 * D].rearrange("p (q c) -> p q c", q=2)
        scrap = chain[:, 1, 2 * D:3 * D]

        def col(n):
            return cvec[:, n:n + 1]
        srmin, nmx, nmx_all, gbias, zmax, zmax_all, zsum, zsum_all, zinv, l1scale, lnb, fac = map(col, range(12))

        tb = [ctx.enter_context(nc.psum_tensor(f"turn{k}", [P, BANK], F32)) for k in range(4)]
        acc_a = [ctx.enter_context(nc.psum_tensor(f"acc_a{b}", [P, BANK], F32)) for b in range(2)]
        acc_b = [ctx.enter_context(nc.psum_tensor(f"acc_b{b}", [P, BANK], F32)) for b in range(2)]
        sc_bank = [tb[0], tb[1], tb[2]]
        tu_bank = [tb[3], acc_a[0], acc_a[1]]
        edge_bank = [[acc_a[0], acc_a[1]], [tb[2], tb[3]]]
        tb16 = [bank[:, :].bitcast(F16) for bank in tb]

        pad_zero = sem("pad_zero")
        x_loaded = [sem(f"x_loaded{n}") for n in range(2)]
        cast_ok = sem("cast_ok")
        w_pow2 = sem("w_pow2")
        w_loaded = sem("w_loaded")
        adj_ready = [sem(f"adj_ready{b}") for b in range(2)]
        adj_pad = sem("adj_pad")
        ident_ok = sem("ident_ok")
        pool_sum = sem("pool_sum")
        w_amax = sem("w_amax")
        w_split = sem("w_split")
        dve = sem("dve")
        var_ok = sem("var_ok")
        sqrt_ok = sem("sqrt_ok")
        norm_ok = sem("norm_ok")
        hn_done = sem("hn_done")
        hn_turned = sem("hn_turned")
        rows_hi = sem("rows_hi")
        rows_lo = sem("rows_lo")
        small_done = sem("small_done")
        nmx_ok = sem("nmx_ok")
        g_ok = sem("g_ok")
        gcol_ok = sem("gcol_ok")
        slb_mm = sem("slb_mm")
        slb_ok = sem("slb_ok")
        v_mm, v_hi_ok, v_lo_ok = sem("v_mm"), sem("v_hi_ok"), sem("v_lo_ok")
        y_mm, y_hi_ok, y_lo_ok = sem("y_mm"), sem("y_hi_ok"), sem("y_lo_ok")
        turn_mm = sem("turn_mm")
        turn_out = sem("turn_out")
        sum_ok = sem("sum_ok")
        relu_ok = sem("relu_ok")
        exp_ok = sem("exp_ok")
        mask_ok = sem("mask_ok")
        num_hi = sem("num_hi")
        num_lo = sem("num_lo")
        y_done = sem("y_done")
        v_done = sem("v_done")
        gate_in = sem("gate_in")
        gate_out = sem("gate_out")
        mix_in = sem("mix_in")
        mix_out = sem("mix_out")
        fin = sem("fin")
        x1_ok = sem("x1_ok")
        st_ok = sem("st_ok")
        edge_mm = sem("edge_mm")
        edge_hi = sem("edge_hi")
        edge_lo = sem("edge_lo")
        supp_mm = sem("supp_mm")
        supp_hi = sem("supp_hi")
        supp_lo = sem("supp_lo")
        z_ok = sem("z_ok")
        zmax_in = sem("zmax_in")
        zneg_ok = sem("zneg_ok")
        zexp_ok = sem("zexp_ok")
        ones_ok = sem("ones_ok")
        mb_ok = sem("mb_ok")
        sc_mm = sem("sc_mm")
        sc_max = sem("sc_max")
        negm_ok = sem("negm_ok")
        sub_ok = sem("sub_ok")
        tu_mm = sem("tu_mm")
        p_hi = sem("p_hi")
        p_ok = sem("p_ok")
        p_lo = sem("p_lo")
        o_mm = sem("o_mm")
        fin1 = sem("fin1")
        keep_ok = sem("keep_ok")
        o_ok = sem("o_ok")
        stored = sem("stored")
        vec_mark, pool_mark = sem("vec_mark"), sem("pool_mark")

        adj_rows = adj[:, :]

        def split_product(pe, psum, parts_l, parts_r, start=True, stop=True):
            n = len(parts_l[0])
            for i, (a, c) in enumerate((a, c) for k in range(n) for a, c in
                                       ((parts_l[0][k], parts_r[0][k]), (parts_l[0][k], parts_r[1][k]),
                                        (parts_l[1][k], parts_r[0][k]))):
                mm = nc.tensor.matmul(psum, a, c, start=(i == 0), stop=(i == 3 * n - 1))
            return mm

        def carry(eng, mark):
            eng.sem_inc(mark, 1)

        def blocks(k):
            return range(k * BPB, min((k + 1) * BPB, T))

        block = ctx.enter_context(nc.Block())

        @block.sync
        def _(sp):
            body = (T - 1) * P
            half = T // 2
            sp.dma_start(xres[:, 0:half, :], x[0:half * P, :].rearrange("(t p) d -> p t d", p=P)).then_inc(x_loaded[0], 16)
            sp.dma_start(xres[:, half:T - 1, :], x[half * P:body, :].rearrange("(t p) d -> p t d", p=P)).then_inc(x_loaded[1], 16)
            sp.wait_ge(pad_zero, 1)
            sp.dma_start(xres[0:TAIL, T - 1, :], x[body:N, :]).then_inc(x_loaded[1], 16)
            sp.wait_ge(w_loaded, 16 * 15)

            def load(t, b, rows=P):
                sp.dma_start(adjr[0:rows, b, 0:N], adj_rows[bass.ds(t * P, rows), :]).then_inc(adj_ready[b], 16)

            load(0, 0)
            load(1, 1)
            with sp.Fori(2, T - 3, 2) as t0:
                for b in range(2):
                    sp.wait_ge(cast_ok, t0 + b - 1)
                    load(t0 + b, b)
            sp.wait_ge(cast_ok, T - 3)
            load(T - 2, 0)
            sp.wait_ge(cast_ok, T - 2)
            load(T - 1, 1, TAIL)
            sp.wait_ge(cast_ok, T - 1)
            load(0, 0)
            sp.wait_ge(cast_ok, T)
            load(1, 1)
            with sp.Fori(2, T - 3, 2) as t0:
                for b in range(2):
                    sp.wait_ge(mb_ok, t0 + b - 1)
                    load(t0 + b, b)
            sp.wait_ge(mb_ok, T - 3)
            load(T - 2, 0)
            sp.wait_ge(mb_ok, T - 2)
            load(T - 1, 1, TAIL)

        @block.gpsimd
        def _(pool):
            nc.gpsimd.memset(ident[:, :], 0.0).then_inc(ident_ok, 1)
            nc.gpsimd.memset(adjr[:, :, N:NP], 0.0).then_inc(adj_pad, 1)
            pool.wait_ge(ident_ok, 1)
            nc.gpsimd.affine_select(out=ident[:, :], in_=ident[:, :], compare_op=ALU.not_equal, fill=1.0,
                                    base=0, pattern=[[-1, P]], channel_multiplier=1).then_inc(ident_ok, 1)
            pool.wait_ge(ident_ok, 2)
            nc.gpsimd.tensor_copy(ident16[:, :], ident[:, :]).then_inc(ident_ok, 1)
            pool.wait_ge(w_amax, 1)
            nc.gpsimd.partition_all_reduce(amax_all[:, :], amax[:, :], P, bass.bass_isa.ReduceOp.max).then_inc(pool_sum, 1)
            pool.wait_ge(w_pow2, 1)
            for g, (c, w) in enumerate(GROUPS):
                nc.gpsimd.tensor_scalar(wall[:, :, c:c + w], wall[:, :, c:c + w], wscale[:, g:g + 1], 1.0,
                                        ALU.mult, ALU.mult).then_inc(w_split, 1)
            pool.wait_ge(w_split, len(GROUPS))
            nc.gpsimd.tensor_scalar(whi[:, :, :], wall[:, :, :], 1.0, 0.0, ALU.mult, ALU.add).then_inc(w_split, 1)
            pool.wait_ge(w_split, len(GROUPS) + 1)
            nc.gpsimd.tensor_tensor(wlo[:, :, :], wall[:, :, :], whi[:, :, :], ALU.subtract).then_inc(w_split, 1)
            pool.wait_ge(w_split, len(GROUPS) + 2)
            for q, part16 in enumerate((whi, wlo)):
                nc.gpsimd.tensor_scalar(urep[:, q], part16[:, :, U_L:U_L + 1].broadcast_to([P, KC, P]), 1.0, 0.0,
                                        ALU.mult, ALU.add).then_inc(w_split, 1)

            def cast(t, b, first=False):
                pool.wait_ge(adj_ready[b], 8 * (t - b) + 16)
                if not first:
                    pool.wait_ge(turn_mm, NG * t)
                carry(pool, pool_mark)
                nc.gpsimd.tensor_scalar(adj16[:, :], adjr[:, b, :], 1.0, 0.0, ALU.mult, ALU.add).then_inc(cast_ok, 1)

            pool.wait_ge(adj_pad, 1)
            cast(0, 0, True)
            pool.wait_ge(nmx_ok, 1)
            nc.gpsimd.partition_all_reduce(nmx_all, nmx, P, bass.bass_isa.ReduceOp.max).then_inc(pool_sum, 1)

            def low(t, b, first):
                pool.wait_ge(num_hi, t + 1)
                if not first:
                    pool.wait_ge(v_done, t - 1)
                nc.gpsimd.tensor_tensor(num[:, b, 1], chain_t[:, b], num[:, b, 0], ALU.subtract).then_inc(num_lo, 1)

            cast(1, 1)
            low(0, 0, True)
            cast(2, 0)
            low(1, 1, True)
            cast(3, 1)
            with pool.Fori(2, T - 3, 2) as t0:
                for b in range(2):
                    low(t0 + b, b, False)
                    cast(t0 + b + 2, b)
            low(T - 2, 0, False)
            low(T - 1, 1, False)

            pool.wait_ge(z_ok, T)
            nc.gpsimd.affine_select(out=nodes[:, T - 1:T], in_=nodes[:, T - 1:T], compare_op=ALU.is_gt,
                                    fill=-MASKED, base=TAIL, pattern=[[0, 1]], channel_multiplier=-1).then_inc(pool_sum, 1)
            pool.wait_ge(zmax_in, 1)
            nc.gpsimd.partition_all_reduce(zmax_all, zmax, P, bass.bass_isa.ReduceOp.max).then_inc(pool_sum, 1)
            pool.wait_ge(zexp_ok, 1)
            nc.gpsimd.partition_all_reduce(zsum_all, zsum, P, bass.bass_isa.ReduceOp.add).then_inc(pool_sum, 1)

            def mask(t, b, first):
                if not first:
                    pool.wait_ge(sc_max, NCH * (t - 1))
                pool.wait_ge(adj_ready[b], 16 * (T // 2) + 8 * (t - b) + 16)
                carry(pool, pool_mark)
                nc.gpsimd.tensor_scalar(maskb[:, b], adjr[:, b, :], MASKED, -MASKED, ALU.mult, ALU.add).then_inc(mb_ok, 1)

            def off(t, b):
                pool.wait_ge(negm_ok, t + 1)
                carry(pool, pool_mark)
                nc.gpsimd.tensor_scalar(chain[:, b, :], chain[:, b, :], negm[:, b:b + 1], 1.0,
                                        ALU.add, ALU.mult).then_inc(sub_ok, 1)

            mask(0, 0, True)
            mask(1, 1, True)
            with pool.Fori(0, T - 3, 2) as t0:
                for b in range(2):
                    off(t0 + b, b)
                    mask(t0 + b + 2, b, False)
            off(T - 2, 0)
            off(T - 1, 1)

        @block.scalar
        def _(act):
            sa_w = [W_sa, W_gcnb, edge_w, weight]
            for n, w in enumerate(sa_w):
                act.dma_start(wall[:, :, n * D:(n + 1) * D], w.rearrange("(k p) c -> p k c", p=P)).then_inc(w_loaded, 16)
            act.dma_start(wall[:, :, ND:ND + 1], node_w.rearrange("(k p) c -> p k c", p=P),
                          allow_slow_non_contiguous=True).then_inc(w_loaded, 16)
            for q in range(2):
                for n, g in enumerate((Wa, Wb)):
                    act.dma_start(wall[:, :, SM + 2 * q + n:SM + 2 * q + n + 1],
                                  g[0:1, q * D:(q + 1) * D].rearrange("o (k p) -> p k o", p=P),
                                  allow_slow_non_contiguous=True).then_inc(w_loaded, 16)
                act.dma_start(arow[:, q, :], a_sa[0, q * D:(q + 1) * D].partition_broadcast(P)).then_inc(w_loaded, 16)
            act.dma_start(bg[:, :], b_gcnb.partition_broadcast(P)).then_inc(w_loaded, 16)
            act.dma_start(bw[:, :], bias.partition_broadcast(P)).then_inc(w_loaded, 16)
            act.dma_start(bab[:, 0:1], ba.partition_broadcast(P)).then_inc(w_loaded, 16)
            act.dma_start(bab[:, 1:2], bb.partition_broadcast(P)).then_inc(w_loaded, 16)

            def norm_and_turn(layer):
                act.wait_ge(var_ok, layer + 1)
                nc.scalar.activation(rstd[:, :], var[:, :], ACT.Sqrt).then_inc(sqrt_ok, 1)
                base = T * layer

                def norm(t, b, first=False):
                    if not first:
                        act.wait_ge(hn_turned, base + t - 1)
                    nc.scalar.activation(hn[:, b, :], xres[:, bass.ds(t, 1), :].squeeze(), ACT.Relu,
                                         bias=shift[:, bass.ds(t, 1)], scale=rstd[:, bass.ds(t, 1)]).then_inc(hn_done, 1)

                def high(t, b):
                    act.wait_ge(hn_turned, base + t + 1)
                    nc.scalar.activation(rows_t[:, 0, :, bass.ds(t * P, P)],
                                         tb[b][:, 0:D].rearrange("p (k n) -> p k n", k=KC), ACT.Copy).then_inc(rows_hi, 1)

                def support_high(t, b):
                    if layer:
                        act.wait_ge(supp_mm, t + 1)
                        nc.scalar.activation(s_hi[:, bass.ds(t, 1), 0:D].squeeze(), acc_b[b][:, 0:D], ACT.Copy,
                                             scale=OUT_SCALE).then_inc(supp_hi, 1)

                act.wait_ge(norm_ok, layer + 1)
                norm(0, 0, True)
                norm(1, 1, True)
                high(0, 0)
                norm(2, 0)
                high(1, 1)
                norm(3, 1)
                with act.Fori(2, T - 3, 2) as t0:
                    for b in range(2):
                        high(t0 + b, b)
                        norm(t0 + b + 2, b)
                        support_high(t0 + b - 2, b)
                for t in (T - 2, T - 1):
                    high(t, t % 2)
                    support_high(t - 2, t % 2)
                support_high(T - 2, 0)
                support_high(T - 1, 1)

            norm_and_turn(0)
            act.wait_ge(g_ok, 1)
            nc.scalar.activation(gcol[:, :], sm[:, :, 4], ACT.Exp, bias=gbias, scale=-0.01).then_inc(gcol_ok, 1)
            nc.scalar.activation(eps_col[:, :], sm[:, :, 5], ACT.Exp, bias=gbias, scale=0.01).then_inc(gcol_ok, 1)

            for k, (c, w) in enumerate(CHUNKS):
                act.wait_ge(slb_mm, k + 1)
                nc.scalar.activation(slb[:, c:c + w], acc_b[k % 2][:, 0:w], ACT.Copy, scale=fac).then_inc(slb_ok, 1)

            act.wait_ge(gcol_ok, 3)

            def proj_high(t, b):
                act.wait_ge(v_mm, t + 1)
                nc.scalar.activation(v_hi[:, bass.ds(t, 1), 0:D].squeeze(), tb[b][:, 0:D], ACT.Copy,
                                     scale=tmp_t[:, bass.ds(t, 1)]).then_inc(v_hi_ok, 1)
                act.wait_ge(y_mm, t + 1)
                nc.scalar.activation(y_hi[:, bass.ds(t, 1), 0:D].squeeze(), tb[2 + b][:, 0:D], ACT.Copy,
                                     scale=OUT_SCALE).then_inc(y_hi_ok, 1)
            with act.Fori(0, T - 1, 2) as t0:
                for b in range(2):
                    proj_high(t0 + b, b)

            def gate_tanh(t, b):
                act.wait_ge(gate_in, t + 1)
                nc.scalar.activation(tg[:, b, :], gates[:, b, :], ACT.Tanh, scale=0.5).then_inc(gate_out, 1)

            def mix_tanh(t, b):
                act.wait_ge(mix_in, t + 1)
                nc.scalar.activation(act_out[:, b, :], mix[:, b, :], ACT.Tanh, scale=0.5).then_inc(mix_out, 1)

            def attend(t, b, early=False):
                if not early:
                    gate_tanh(t - 2, b)
                act.wait_ge(relu_ok, t + 1)
                nc.scalar.activation(chain[:, b, :], chain[:, b, :], ACT.Exp, scale=-0.99).then_inc(exp_ok, 1)
                for g, (m, n) in enumerate(GROUPS_T):
                    act.wait_ge(turn_mm, NG * t + g + 1)
                    if g == 0 and not early:
                        act.wait_ge(y_done, t - 1)
                        act.wait_ge(mask_ok, t - 1)
                    nc.scalar.activation(adj_t[:, b, m:m + n].rearrange("p t i -> p (t i)"), tb16[g][:, 0:n * P],
                                         ACT.Copy).then_inc(turn_out, 1)
                    if g == 1 and not early:
                        mix_tanh(t - 2, b)
                act.wait_ge(mask_ok, t + 1)
                if not early:
                    act.wait_ge(v_done, t - 1)
                nc.scalar.activation(num[:, b, 0], chain_t[:, b], ACT.Copy).then_inc(num_hi, 1)

            attend(0, 0, True)
            attend(1, 1, True)
            with act.Fori(2, T - 1, 2) as t0:
                for b in range(2):
                    attend(t0 + b, b)
            for t in (T - 2, T - 1):
                gate_tanh(t, t % 2)
                mix_tanh(t, t % 2)

            norm_and_turn(1)

            def edge_high(k, c, w, par):
                for m in range(KC):
                    act.wait_ge(edge_mm, KC * k + m + 1)
                    nc.scalar.activation(eh_t[0][:, m, bass.ds(c, w)], edge_bank[par][m][:, 0:w], ACT.Copy,
                                         scale=OUT_SCALE).then_inc(edge_hi, 1)
            with act.Fori(0, NCH - 2, 2) as k0:
                for par in range(2):
                    edge_high(k0 + par, (k0 + par) * BANK, BANK, par)
            edge_high(NCH - 1, *CHUNKS[-1], 0)
            act.wait_ge(zneg_ok, 1)
            nc.scalar.activation(nodes[:, :], nodes[:, :], ACT.Exp, bias=zmax_all, accum_out=zsum).then_inc(zexp_ok, 1)

            def numer(t, b, first):
                for k, (c, w) in enumerate(CHUNKS):
                    act.wait_ge(tu_mm, NCH * t + k + 1)
                    if k == 0 and not first:
                        act.wait_ge(o_mm, t - 1)
                    nc.scalar.activation(num[:, b, 0].rearrange("p t i -> p (t i)")[:, c:c + w], tu_bank[k % 3][:, 0:w],
                                         ACT.Exp, bias=lnb, scale=l1scale).then_inc(p_hi, 1)
                    if not (first and t == 0):
                        act.wait_ge(p_lo, NCH * (t - 1) + k + 1)
                    nc.scalar.activation(pnum[:, c:c + w], tu_bank[k % 3][:, 0:w], ACT.Exp, bias=lnb,
                                         scale=l1scale).then_inc(p_ok, 1)

            numer(0, 0, True)
            numer(1, 1, True)
            with act.Fori(2, T - 1, 2) as t0:
                for b in range(2):
                    numer(t0 + b, b, False)
                    act.wait_ge(o_ok, t0 + b - 1)
                    act.dma_start(out[bass.ds((t0 + b - 2) * P, P), :],
                                  xres[:, bass.ds(t0 + b - 2, 1), :].squeeze()).then_inc(stored, 16)
            act.wait_ge(o_ok, T - 1)
            act.dma_start(out[(T - 2) * P:(T - 1) * P, :], xres[:, T - 2, :]).then_inc(stored, 16)
            act.wait_ge(o_ok, T)
            act.dma_start(out[(T - 1) * P:N, :], xres[0:TAIL, T - 1, :]).then_inc(stored, 16)
            act.wait_ge(stored, 16 * T)

        @block.vector
        def _(vec):
            count = [0]

            def step(ins):
                count[0] += 1
                ins.then_inc(dve, 1)
                vec.wait_ge(dve, count[0])

            v = nc.vector
            v.memset(xres[96:P, T - 1, :], 0.0).then_inc(pad_zero, 1)
            step(v.memset(lnb, LN_EXP_SCALE))
            step(v.memset(wall[:, :, WCOLS - 1:WCOLS], 0.0))
            vec.wait_ge(w_loaded, 16 * 15)
            for k in range(KC):
                for q, c in ((1, U_R), (0, U_L)):
                    step(v.tensor_tensor_reduce(out=scrap, in0=wall[:, k, SA:SA + D], in1=arow[:, q, :], scale=1.0,
                                                scalar=0.0, op0=ALU.mult, op1=ALU.add, accum_out=wall[:, k, c:c + 1]))
            for g, (c, w) in enumerate(GROUPS):
                step(v.tensor_reduce(amax[:, g:g + 1], wall[:, :, c:c + w], XY, ALU.max, apply_absolute_value=True))
            step(v.tensor_scalar(amax[:, :], amax[:, :], 1e-30, None, ALU.max))
            v.nop().then_inc(w_amax, 1)

            def row_stats(t0, n):
                for b in range(n):
                    v.bn_stats(stats[:, bass.ds(t0 + b, 1), :].squeeze(),
                               xres[:, bass.ds(t0 + b, 1), :].squeeze()).then_inc(st_ok, 1)
            half = T // 2
            vec.wait_ge(x_loaded[0], 16)
            with vec.Fori(0, half - 4, 4) as t0:
                row_stats(t0, 4)
            row_stats(half - 1, 1)
            vec.wait_ge(x_loaded[1], 32)
            with vec.Fori(half, T - 4, 4) as t0:
                row_stats(t0, 4)
            row_stats(T - 1, 1)

            vec.wait_ge(pool_sum, 1)
            step(v.tensor_scalar(pow2[:, :].bitcast(U32), amax_all[:, :].bitcast(U32), 0x7F800000, None, ALU.bitwise_and))
            step(v.reciprocal(wscale[:, :], pow2[:, :]))
            step(v.tensor_scalar(wscale[:, :], wscale[:, :], W_TOP, None, ALU.mult))
            v.nop().then_inc(w_pow2, 1)
            step(v.tensor_scalar(unsc[:, :], pow2[:, :], UNSCALE, None, ALU.mult))
            step(v.tensor_tensor(l1scale, unsc[:, G_ED:G_ED + 1], unsc[:, G_ED:G_ED + 1], ALU.mult))

            def norm_stats(layer):
                step(v.tensor_tensor(mean[:, :], stats[:, :, 1], stats[:, :, 4], ALU.add))
                step(v.tensor_tensor(tmp_t[:, :], stats[:, :, 1], stats[:, :, 4], ALU.subtract))
                step(v.tensor_scalar(mean[:, :], mean[:, :], 0.5, None, ALU.mult))
                step(v.tensor_tensor(tmp_t[:, :], tmp_t[:, :], tmp_t[:, :], ALU.mult))
                step(v.tensor_tensor(var[:, :], stats[:, :, 2], stats[:, :, 5], ALU.add))
                step(v.tensor_scalar(tmp_t[:, :], tmp_t[:, :], 0.25, EPS_LN, ALU.mult, ALU.add))
                step(v.scalar_tensor_tensor(out=var[:, :], in0=var[:, :], scalar=1.0 / D, in1=tmp_t[:, :],
                                            op0=ALU.mult, op1=ALU.add))
                v.nop().then_inc(var_ok, 1)
                vec.wait_ge(sqrt_ok, layer + 1)
                step(v.reciprocal(rstd[:, :], rstd[:, :]))
                step(v.tensor_tensor(tmp_t[:, :], rstd[:, :], rstd[:, :], ALU.mult))
                step(v.tensor_tensor(tmp_t[:, :], tmp_t[:, :], var[:, :], ALU.mult))
                step(v.tensor_scalar(tmp_t[:, :], tmp_t[:, :], -0.5 * H_SCALE, 1.5 * H_SCALE, ALU.mult, ALU.add))
                step(v.tensor_tensor(rstd[:, :], rstd[:, :], tmp_t[:, :], ALU.mult))
                step(v.scalar_tensor_tensor(out=shift[:, :], in0=mean[:, :], scalar=-1.0, in1=rstd[:, :],
                                            op0=ALU.mult, op1=ALU.mult))
                v.nop().then_inc(norm_ok, 1)

            def rows_low(layer):
                def low(t, b):
                    vec.wait_ge(rows_hi, T * layer + t + 1)
                    v.tensor_tensor(rows_t[:, 1, :, bass.ds(t * P, P)], tb[b][:, 0:D].rearrange("p (k n) -> p k n", k=KC),
                                    rows_t[:, 0, :, bass.ds(t * P, P)], ALU.subtract).then_inc(rows_lo, 1)

                def support_low(t, b):
                    if layer:
                        vec.wait_ge(supp_hi, t + 1)
                        v.tensor_scalar(nodes[:, bass.ds(t, 1)], acc_b[b][:, D:D + 1], fac, None, ALU.mult).then_inc(z_ok, 1)
                        v.scalar_tensor_tensor(out=s_lo[:, bass.ds(t, 1), 0:D].squeeze(), in0=acc_b[b][:, 0:D],
                                               scalar=OUT_SCALE, in1=s_hi[:, bass.ds(t, 1), 0:D].squeeze(),
                                               op0=ALU.mult, op1=ALU.subtract).then_inc(supp_lo, 1)

                low(0, 0)
                low(1, 1)
                with vec.Fori(2, T - 1, 2) as t0:
                    for b in range(2):
                        low(t0 + b, b)
                        support_low(t0 + b - 2, b)
                support_low(T - 2, 0)
                support_low(T - 1, 1)

            vec.wait_ge(st_ok, T)
            norm_stats(0)
            rows_low(0)

            vec.wait_ge(small_done, T)
            small = acc_a[0][:, 0:8 * T].rearrange("p (t c) -> p t c", c=8)
            v.tensor_scalar(fac, unsc[:, G_SM:G_SM + 1], OUT_SCALE, None, ALU.mult).then_inc(dve, 1)
            count[0] += 1
            vec.wait_ge(dve, count[0])
            step(v.tensor_scalar(sm[:, :, :], small[:, :, 0:6], fac, None, ALU.mult))
            for n in range(2):
                step(v.tensor_scalar(rab[:, :, n], sm[:, :, 2 + n], bab[:, n:n + 1], None, ALU.add))
            step(v.tensor_reduce(srmin, sm[:, :, 4], X, ALU.min))
            step(v.tensor_scalar(nmx, srmin, -1.0, None, ALU.mult))
            v.nop().then_inc(nmx_ok, 1)
            step(v.tensor_scalar(sm[:, :, 2:4], small[:, :, 0:2], OUT_SCALE, None, ALU.mult))
            step(v.tensor_copy(y_hi[:, :, D:D + 2], sm[:, :, 2:4]))
            step(v.tensor_tensor(y_lo[:, :, D:D + 2], sm[:, :, 2:4], y_hi[:, :, D:D + 2], ALU.subtract))
            vec.wait_ge(pool_sum, 2)
            step(v.tensor_scalar(gbias, nmx_all, -0.01, None, ALU.mult))
            v.nop().then_inc(g_ok, 1)
            vec.wait_ge(gcol_ok, 2)
            step(v.tensor_scalar(eps_col[:, :], eps_col[:, :], EPS_ATT * G_SCALE, None, ALU.mult))
            step(v.tensor_scalar(tmp_t[:, :], gcol[:, :], G_SCALE, None, ALU.mult))
            step(v.tensor_copy(v_hi[:, :, D], tmp_t[:, :]))
            step(v.tensor_tensor(v_lo[:, :, D], tmp_t[:, :], v_hi[:, :, D], ALU.subtract))
            step(v.tensor_scalar(tmp_t[:, :], gcol[:, :], OUT_SCALE, None, ALU.mult))
            v.nop().then_inc(gcol_ok, 1)
            step(v.tensor_copy(srt[:, :], sm[:, :, 4]))

            with vec.Fori(0, T - 1, 2) as t0:
                for b in range(2):
                    t = t0 + b
                    vec.wait_ge(v_hi_ok, t + 1)
                    v.scalar_tensor_tensor(out=v_lo[:, bass.ds(t, 1), 0:D].squeeze(), in0=tb[b][:, 0:D],
                                           scalar=tmp_t[:, bass.ds(t, 1)], in1=v_hi[:, bass.ds(t, 1), 0:D].squeeze(),
                                           op0=ALU.mult, op1=ALU.subtract).then_inc(v_lo_ok, 1)
                    vec.wait_ge(y_hi_ok, t + 1)
                    v.scalar_tensor_tensor(out=y_lo[:, bass.ds(t, 1), 0:D].squeeze(), in0=tb[2 + b][:, 0:D],
                                           scalar=OUT_SCALE, in1=y_hi[:, bass.ds(t, 1), 0:D].squeeze(),
                                           op0=ALU.mult, op1=ALU.subtract).then_inc(y_lo_ok, 1)
            vec.wait_ge(slb_ok, NCH)
            step(v.tensor_scalar(fac, unsc[:, G_SA:G_SA + 1], G_SCALE, None, ALU.mult))

            FIN = 9

            def finish_a(t, b):
                vec.wait_ge(v_done, t + 1)
                v.scalar_tensor_tensor(out=gates[:, b, :], in0=acc_a[b][:, D:D + 2], scalar=unsc[:, G_SM:G_SM + 1],
                                       in1=rab[:, bass.ds(t, 1), :].squeeze(), op0=ALU.mult, op1=ALU.add).then_inc(gate_in, 1)
                v.tensor_scalar(den[:, b, 0:1], acc_b[b][:, D:D + 1], eps_col[:, bass.ds(t, 1)], None,
                                ALU.add).then_inc(fin, 1)
                v.scalar_tensor_tensor(out=mix[:, b, :], in0=acc_a[b][:, 0:D], scalar=unsc[:, G_GC:G_GC + 1],
                                       in1=bg[:, :], op0=ALU.mult, op1=ALU.add).then_inc(fin, 1)
                vec.wait_ge(fin, FIN * t + 1)
                v.reciprocal(den[:, b, 1:2], den[:, b, 0:1]).then_inc(fin, 1)

            def finish_b(t, b):
                vec.wait_ge(gate_out, t + 1)
                v.tensor_scalar(tg[:, b, :], tg[:, b, :], 0.5, 0.5, ALU.mult, ALU.add).then_inc(fin, 1)
                vec.wait_ge(fin, FIN * t + 4)
                v.tensor_scalar(den[:, b, 2:3], tg[:, b, 0:1], den[:, b, 1:2], fac, ALU.mult, ALU.mult).then_inc(fin, 1)
                v.tensor_scalar(mix[:, b, :], mix[:, b, :], tg[:, b, 1:2], None, ALU.mult).then_inc(fin, 1)
                vec.wait_ge(fin, FIN * t + 6)
                v.scalar_tensor_tensor(out=mix[:, b, :], in0=acc_b[b][:, 0:D], scalar=den[:, b, 2:3],
                                       in1=mix[:, b, :], op0=ALU.mult, op1=ALU.add).then_inc(mix_in, 1)

            def finish_c(t, b):
                vec.wait_ge(mix_out, t + 1)
                v.tensor_scalar(act_out[:, b, :], act_out[:, b, :], 0.5, 0.5, ALU.mult, ALU.add).then_inc(fin, 1)
                vec.wait_ge(fin, FIN * t + 7)
                xt = xres[:, bass.ds(t, 1), :].squeeze()
                v.tensor_tensor(xt, act_out[:, b, :], xt, ALU.add).then_inc(fin, 1)
                vec.wait_ge(fin, FIN * t + 8)
                v.bn_stats(stats[:, bass.ds(t, 1), :].squeeze(), xt).then_inc(fin, 1)

            def attend(t, b, early=False):
                if not early:
                    vec.wait_ge(num_lo, t - 1)
                v.tensor_tensor(chain_t[:, b], slb[:, bass.ds(t * P, P)].unsqueeze(1).broadcast_to([P, T, P]),
                                srt[:, :].unsqueeze(2).broadcast_to([P, T, P]), ALU.add).then_inc(sum_ok, 1)
                vec.wait_ge(sum_ok, t + 1)
                v.tensor_scalar(chain[:, b, :], chain[:, b, :], 0.0, None, ALU.max).then_inc(relu_ok, 1)
                if not early:
                    finish_a(t - 2, b)
                    finish_b(t - 2, b)
                    finish_c(t - 2, b)
                vec.wait_ge(exp_ok, t + 1)
                vec.wait_ge(turn_out, NG * (t + 1))
                v.tensor_tensor(chain_t[:, b], chain_t[:, b], adj_t[:, b], ALU.mult).then_inc(mask_ok, 1)

            attend(0, 0, True)
            attend(1, 1, True)
            with vec.Fori(2, T - 1, 2) as t0:
                for b in range(2):
                    attend(t0 + b, b)
            for t in (T - 2, T - 1):
                finish_a(t, t % 2)
                finish_b(t, t % 2)
                finish_c(t, t % 2)

            vec.wait_ge(fin, FIN * T)
            step(v.tensor_scalar(fac, unsc[:, G_ND:G_ND + 1], OUT_SCALE, None, ALU.mult))
            norm_stats(1)
            rows_low(1)

            def edge_low(k, c, w, par):
                for m in range(KC):
                    vec.wait_ge(edge_hi, KC * k + m + 1)
                    v.scalar_tensor_tensor(out=eh_t[1][:, m, bass.ds(c, w)], in0=edge_bank[par][m][:, 0:w],
                                           scalar=OUT_SCALE, in1=eh_t[0][:, m, bass.ds(c, w)], op0=ALU.mult,
                                           op1=ALU.subtract).then_inc(edge_lo, 1)
            with vec.Fori(0, NCH - 2, 2) as k0:
                for par in range(2):
                    edge_low(k0 + par, (k0 + par) * BANK, BANK, par)
            edge_low(NCH - 1, *CHUNKS[-1], 0)
            step(v.memset(s_hi[:, :, D:CV], 1.0))
            step(v.memset(s_lo[:, :, D:CV], 0.0))
            v.nop().then_inc(ones_ok, 1)
            vec.wait_ge(pool_sum, 3)
            step(v.tensor_reduce(zmax, nodes[:, :], X, ALU.max))
            v.nop().then_inc(zmax_in, 1)
            vec.wait_ge(pool_sum, 4)
            step(v.tensor_scalar(zmax_all, zmax_all, -1.0, None, ALU.mult))
            v.nop().then_inc(zneg_ok, 1)
            vec.wait_ge(pool_sum, 5)
            step(v.reciprocal(zinv, zsum_all))
            step(v.tensor_scalar(nodes[:, :], nodes[:, :], zinv, unsc[:, G_WT:G_WT + 1], ALU.mult, ALU.mult))

            F1 = 3

            def scan(t, b, k, c, w, first):
                if k == 0:
                    vec.wait_ge(mb_ok, t + 1)
                    if not first:
                        vec.wait_ge(tu_mm, NCH * (t - 1))
                vec.wait_ge(sc_mm, NCH * t + k + 1)
                carry(vec, vec_mark)
                v.tensor_tensor_reduce(out=chain[:, b, c:c + w], in0=sc_bank[k % 3][:, 0:w], in1=maskb[:, b, c:c + w],
                                       scale=1.0, scalar=-3.0e38, op0=ALU.add, op1=ALU.max,
                                       accum_out=cmax[:, b, k:k + 1]).then_inc(sc_max, 1)

            def top(t, b):
                vec.wait_ge(sc_max, NCH * (t + 1))
                v.tensor_reduce(negm[:, b:b + 1], cmax[:, b, 0:NCH], X, ALU.max, negate=True).then_inc(negm_ok, 1)

            def low(t, b, k, c, w):
                vec.wait_ge(p_ok, NCH * t + k + 1)
                if k == 0:
                    pass
                v.tensor_tensor(num[:, b, 1].rearrange("p t i -> p (t i)")[:, c:c + w], pnum[:, c:c + w],
                                num[:, b, 0].rearrange("p t i -> p (t i)")[:, c:c + w], ALU.subtract).then_inc(p_lo, 1)

            def keep(t, b):
                vec.wait_ge(negm_ok, t + 1)
                v.tensor_scalar(den[:, b, 3:4], negm[:, b:b + 1], 0.5 * MASKED, None, ALU.is_lt).then_inc(keep_ok, 1)

            def finish(t, b):
                vec.wait_ge(o_mm, t + 1)
                v.reciprocal(den[:, b, 0:1], acc_b[b][:, D:D + 1]).then_inc(fin1, 1)
                vec.wait_ge(fin1, F1 * t + 1)
                vec.wait_ge(keep_ok, t + 1)
                v.tensor_scalar(den[:, b, 1:2], den[:, b, 0:1], nodes[:, bass.ds(t, 1)], den[:, b, 3:4],
                                ALU.mult, ALU.mult).then_inc(fin1, 1)
                vec.wait_ge(fin1, F1 * t + 2)
                xt = xres[:, bass.ds(t, 1), :].squeeze()
                v.scalar_tensor_tensor(out=mix[:, b, :], in0=acc_b[b][:, 0:D], scalar=den[:, b, 1:2], in1=xt,
                                       op0=ALU.mult, op1=ALU.add).then_inc(fin1, 1)
                vec.wait_ge(fin1, F1 * t + 3)
                v.tensor_tensor(xt, mix[:, b, :], bw[:, :], ALU.add).then_inc(o_ok, 1)

            def tile(t, b, first=False, last=False, before=True):
                keep(t, b)
                for k, (c, w) in enumerate(CHUNKS):
                    if not last:
                        scan(t + 1, 1 - b, k, c, w, first)
                    low(t, b, k, c, w)
                    if k == 2 and before:
                        finish(t - 1, 1 - b)
                if not last:
                    top(t + 1, 1 - b)

            for k, (c, w) in enumerate(CHUNKS):
                scan(0, 0, k, c, w, True)
            top(0, 0)
            vec.wait_ge(negm_ok, 1)
            tile(0, 0, first=True, before=False)
            tile(1, 1)
            with vec.Fori(2, T - 3, 2) as t0:
                for b in range(2):
                    tile(t0 + b, b)
            tile(T - 2, 0)
            tile(T - 1, 1, last=True)
            finish(T - 1, 1)

        @block.tensor
        def _(pe):
            pe.wait_ge(ident_ok, 3)

            def lhs(t):
                return [[rows_t[:, q, k, bass.ds(t * P, P)] for k in range(KC)] for q in range(2)]

            def wcols(c, w):
                return [[m[:, k, c:c + w] for k in range(KC)] for m in (whi, wlo)]

            def rows_turned(layer):
                base = T * layer

                def turn(t, b, first=False):
                    pe.wait_ge(hn_done, base + t + 1)
                    if not first:
                        pe.wait_ge(rows_lo, base + t - 1)
                    for k in range(KC):
                        tr = nc.tensor.transpose(tb[b][:, k * P:(k + 1) * P], hn[:, b, k * P:(k + 1) * P], ident[:, :])
                    tr.then_inc(hn_turned, 1)

                def use(t, b, first=False):
                    pe.wait_ge(rows_lo, base + t + 1)
                    if not layer:
                        split_product(pe, acc_a[0][:, bass.ds(t * 8, 6)], lhs(t), wcols(SM, 6)).then_inc(small_done, 1)
                        return
                    if not first:
                        pe.wait_ge(supp_lo, t - 1)
                    split_product(pe, acc_b[b][:, 0:D + 1], lhs(t), wcols(WT, D + 1)).then_inc(supp_mm, 1)

                turn(0, 0, True)
                turn(1, 1, True)
                if not layer:
                    pe.wait_ge(w_split, len(GROUPS) + 4)
                turn(2, 0)
                use(0, 0, True)
                turn(3, 1)
                use(1, 1, True)
                with pe.Fori(4, T - 1, 2) as t0:
                    for b in range(2):
                        turn(t0 + b, b)
                        use(t0 + b - 2, b)
                use(T - 2, 0)
                use(T - 1, 1)

            rows_turned(0)
            for k, (c, w) in enumerate(CHUNKS):
                if k >= 2:
                    pe.wait_ge(slb_ok, k - 1)
                split_product(pe, acc_b[k % 2][:, 0:w], [[urep[:, q, m] for m in range(KC)] for q in range(2)],
                              [[rows_t[:, q, m, c:c + w] for m in range(KC)] for q in range(2)]).then_inc(slb_mm, 1)

            def project(t, b, first=False):
                if not first:
                    pe.wait_ge(v_lo_ok, t - 1)
                split_product(pe, tb[b][:, 0:D], lhs(t), wcols(SA, D)).then_inc(v_mm, 1)
                if not first:
                    pe.wait_ge(y_lo_ok, t - 1)
                split_product(pe, tb[2 + b][:, 0:D], lhs(t), wcols(GC, D)).then_inc(y_mm, 1)
            project(0, 0, True)
            project(1, 1, True)
            with pe.Fori(2, T - 1, 2) as t0:
                for b in range(2):
                    project(t0 + b, b)
            pe.wait_ge(y_lo_ok, T)

            def turn(t, g, first=False):
                if g == 0:
                    pe.wait_ge(cast_ok, t + 1)
                if not first:
                    pe.wait_ge(turn_out, NG * (t - 1) + g + 1)
                m, n = GROUPS_T[g]
                for j in range(n):
                    tr = nc.tensor.transpose(tb16[g][:, j * P:(j + 1) * P], adj16[:, (m + j) * P:(m + j + 1) * P],
                                             ident16[:, :])
                tr.then_inc(turn_mm, 1)

            def attend(t, b, early=False, last=False):
                if not early:
                    pe.wait_ge(mix_in, t - 1)
                for g, (m0, n) in enumerate(GROUPS_T):
                    if not last:
                        turn(t + 1, g)
                    pe.wait_ge(turn_out, NG * t + g + 1)
                    for m in range(m0, m0 + n):
                        for q, y in enumerate((y_hi, y_lo)):
                            mm = nc.tensor.matmul(acc_a[b][:, 0:CV], adj_t[:, b, m], y[:, m, :],
                                                  start=(m == 0 and q == 0), stop=(m == T - 1 and q == 1))
                mm.then_inc(y_done, 1)
                pe.wait_ge(num_hi, t + 1)
                for m in range(T):
                    for q, y in enumerate((v_hi, v_lo)):
                        nc.tensor.matmul(acc_b[b][:, 0:D + 1], num[:, b, 0, m], y[:, m, 0:D + 1],
                                         start=(m == 0 and q == 0), stop=False)
                pe.wait_ge(num_lo, t + 1)
                for m in range(T):
                    mm = nc.tensor.matmul(acc_b[b][:, 0:D + 1], num[:, b, 1, m], v_hi[:, m, 0:D + 1],
                                          start=False, stop=(m == T - 1))
                mm.then_inc(v_done, 1)

            for g in range(NG):
                turn(0, g, first=True)
            attend(0, 0, early=True)
            attend(1, 1, early=True)
            with pe.Fori(2, T - 3, 2) as t0:
                for b in range(2):
                    attend(t0 + b, b)
            attend(T - 2, 0)
            attend(T - 1, 1, last=True)

            pe.wait_ge(mix_in, T)
            rows_turned(1)

            def edge(k, c, w, par, first=False):
                for m in range(KC):
                    if not first:
                        pe.wait_ge(edge_lo, KC * (k - 2) + m + 1)
                    split_product(pe, edge_bank[par][m][:, 0:w], wcols(ED + m * P, P),
                                  [[rows_t[:, q, j, bass.ds(c, w)] for j in range(KC)] for q in range(2)]).then_inc(edge_mm, 1)

            edge(0, 0, BANK, 0, first=True)
            edge(1, BANK, BANK, 1, first=True)
            with pe.Fori(2, NCH - 2, 2) as k0:
                for par in range(2):
                    edge(k0 + par, (k0 + par) * BANK, BANK, par)
            edge(NCH - 1, *CHUNKS[-1], 0)
            pe.wait_ge(edge_lo, KC * NCH)
            pe.wait_ge(supp_lo, T)
            pe.wait_ge(ones_ok, 1)

            def score(t, k, c, w, first=False):
                if not (first and k < 3):
                    prev = {0: 6, 1: 4, 2: 5}[k] + 1 - NCH if k < 3 else k - 2
                    pe.wait_ge(sc_max, NCH * t + prev)
                split_product(pe, sc_bank[k % 3][:, 0:w], [[eh_t[q][:, j, bass.ds(t * P, P)] for j in range(KC)] for q in range(2)],
                              [[eh_t[q][:, j, c:c + w] for j in range(KC)] for q in range(2)]).then_inc(sc_mm, 1)

            def turn_scores(t, b, k, first=False):
                if k == 0:
                    pe.wait_ge(sub_ok, t + 1)
                if not (first and k < 3):
                    prev = {0: 6, 1: 4, 2: 5}[k] + 1 - NCH if k < 3 else k - 2
                    pe.wait_ge(p_ok, NCH * t + prev)
                for j, m in enumerate(blocks(k)):
                    tr = nc.tensor.transpose(tu_bank[k % 3][:, j * P:(j + 1) * P], chain_t[:, b, m], ident[:, :])
                tr.then_inc(tu_mm, 1)

            def rows_out(t, b, first=False):
                if not first:
                    pe.wait_ge(fin1, F1 * (t - 1))
                for k in range(NCH):
                    pe.wait_ge(p_lo, NCH * t + k + 1)
                    for m in blocks(k):
                        for a, s in ((0, s_hi), (0, s_lo), (1, s_hi)):
                            mm = nc.tensor.matmul(acc_b[b][:, 0:D + 1], num[:, b, a, m], s[:, m, 0:D + 1],
                                                  start=(m == 0 and a == 0 and s is s_hi), stop=(m == T - 1 and a == 1))
                mm.then_inc(o_mm, 1)

            def tile(t, b, first=False, last=False, early=False):
                for k, (c, w) in enumerate(CHUNKS):
                    if not last:
                        score(t + 1, k, c, w)
                    turn_scores(t, b, k, first)
                rows_out(t, b, early)

            F1 = 3
            for k, (c, w) in enumerate(CHUNKS):
                score(0, k, c, w, True)
            tile(0, 0, first=True, early=True)
            tile(1, 1, early=True)
            with pe.Fori(2, T - 3, 2) as t0:
                for b in range(2):
                    tile(t0 + b, b)
            tile(T - 2, 0)
            tile(T - 1, 1, last=True)


_INS = ['x', 'adj', 'L0_gnn_W_sa', 'L0_gnn_a_sa', 'L0_gnn_W_gcnb', 'L0_gnn_b_gcnb', 'L0_gnn_Wa', 'L0_gnn_ba',
        'L0_gnn_Wb', 'L0_gnn_bb', 'L1_gnn_weight', 'L1_gnn_bias', 'L1_gnn_node_w', 'L1_gnn_edge_w']


def kernel(**inputs):
    import numpy as _np
    import concourse.bacc as _bacc
    from concourse import mybir as _mybir
    from concourse.bass_utils import run_bass_kernel_spmd as _run

    nc = _bacc.Bacc("TRN2", target_bir_lowering=False, num_devices=1)
    arrays, args = {}, []
    for name in _INS:
        a = _np.ascontiguousarray(inputs[name])
        arrays[f"in_{name}"] = a
        args.append(nc.dram_tensor(f"in_{name}", a.shape, _mybir.dt.from_np(a.dtype), kind="ExternalInput").ap())
    out = nc.dram_tensor("out_x", inputs['x'].shape, _mybir.dt.float32, kind="ExternalOutput").ap()
    build(nc, *args, out)
    r = _run(nc, [arrays], core_ids=[0])
    return r.results[0]["out_x"]
```

```python
from contextlib import ExitStack

import concourse.bass as bass
from concourse import mybir
from concourse.alu_op_type import AluOpType as ALU

ACT = mybir.ActivationFunctionType
F32, F16, BF16, U32, I32 = mybir.dt.float32, mybir.dt.float16, mybir.dt.bfloat16, mybir.dt.uint32, mybir.dt.int32
X, XY = mybir.AxisListType.X, mybir.AxisListType.XY

P = 128
BANK = 512
H_SCALE = 16.0
W_TOP = 64.0
OUT_SCALE = 1.0 / 16.0
UNSCALE = 1.0 / (H_SCALE * W_TOP * OUT_SCALE)
G_SCALE = 1024.0
MASKED = 1.0e30
LN_EXP_SCALE = 8.317766166719343
EPS_LN, EPS_ATT = 1e-5, 1e-5
RSQRT_BITS = 1597463007.0

SA, GC, ED, WT, ND, SM = 0, 256, 512, 768, 1024, 1025
WCOLS = 1032
GROUPS = [(SA, 256), (GC, 256), (ED, 256), (WT, 256), (ND, 1), (SM, 6)]
SPLITS = [(ND, 7), (GC, 256), (SA, 256), (ED, 512)]
G_SA, G_GC, G_ED, G_WT, G_ND, G_SM = range(6)
U_R, U_L = SM + 4, SM + 5


def build(nc, x, adj, W_sa, a_sa, W_gcnb, b_gcnb, Wa, ba, Wb, bb, weight, bias, node_w, edge_w, out):
    N, D = x.shape
    KC = D // P
    T = -(-N // P)
    NP = T * P
    TAIL = N - (T - 1) * P
    assert D == 256 and T % 2 == 0 and 0 < TAIL < P
    CHUNKS = [(c, min(BANK, NP - c)) for c in range(0, NP, BANK)]
    NCH = len(CHUNKS)
    CV = D + 2
    BPB = BANK // P
    GROUPS_T = [(g, min(2 * BPB, T - g)) for g in range(0, T, 2 * BPB)]
    NG = len(GROUPS_T)
    X_PARTS = [(0, 6), (6, 6), (12, 6), (18, T - 18)]
    W_LOADS, SMALL_LOADS = 6, 5
    RB = 4
    LOOPED = (T - RB) // RB * RB
    SUP = 4
    assert NG == 4 and NCH == 7 and RB == BPB and SUP == RB
    PAIRS = T // 2
    SB = 4
    assert PAIRS % 2 == 1 and PAIRS > 2 * SB

    with ExitStack() as ctx:
        def sb(name, shape, dt=F32):
            return ctx.enter_context(nc.sbuf_tensor(name, shape, dt))

        def sem(name):
            return ctx.enter_context(nc.semaphore(name))

        xres = sb("xres", [P, T, D])
        ident = sb("ident", [P, P])
        ident16 = sb("ident16", [P, P], F16)
        wide = sb("wide", [P, NP + 2 * KC * WCOLS], F16)
        adj16 = wide[:, 0:NP]
        whi, wlo = (wide[:, NP + q * KC * WCOLS:NP + (q + 1) * KC * WCOLS].rearrange("p (k c) -> p k c", k=KC)
                    for q in range(2))
        bg = sb("bg", [P, D])
        bw = sb("bw", [P, D])
        mix = sb("mix", [P, 2, D])
        act_out = sb("act_out", [P, 2, D])
        stats = sb("stats", [P, T, 6])
        mean = sb("mean", [P, T])
        var = sb("var", [P, T])
        rstd = sb("rstd", [P, T])
        tmp_t = sb("tmp_t", [P, T])
        tmp_n = sb("tmp_n", [P, T])
        shift = sb("shift", [P, T])
        sm = sb("sm", [P, T, 6])
        rab = sb("rab", [P, T, 2])
        eps_col = sb("eps_col", [P, T])
        srt = sb("srt", [P, T])
        gcol = sb("gcol", [P, T])
        nodes = sb("nodes", [P, T])
        amax = sb("amax", [P, 6])
        amax_all = sb("amax_all", [P, 6])
        pow2 = sb("pow2", [P, 6])
        wscale = sb("wscale", [P, 6])
        unsc = sb("unsc", [P, 6])
        cvec = sb("cvec", [P, 14])
        gates = sb("gates", [P, 2, 2])
        tg = sb("tg", [P, 2, 2])
        den = sb("den", [P, 2, 4])
        negm = sb("negm", [P, 2, 2])
        bab = sb("bab", [P, 2])
        yv = sb("yv", [P, 4 * T * CV // 2])
        slb = sb("slb", [P, NP])
        adjr = sb("adjr", [P, 2, NP])
        hn = [slb[:, 0:RB * D].rearrange("p (b d) -> p b d", b=RB),
              adj16[:, 0:2 * RB * D].bitcast(F32).rearrange("p (b d) -> p b d", b=RB)]
        adjt = sb("adjt", [P, 2, NP // 2])
        chain = sb("chain", [P, 2, NP])
        ehl = sb("ehl", [P, 2, NP])

        yv16 = yv[:, :].bitcast(F16)
        span = T * CV
        part = [yv16[:, q * span:(q + 1) * span].rearrange("p (t c) -> p t c", c=CV) for q in range(4)]
        y_hi, y_lo, v_hi, v_lo = part
        s_hi, s_lo = part[0], part[1]
        turned = yv16[:, 2 * span:2 * span + 2 * KC * NP].rearrange("p (q k n) -> p q k n", q=2, k=KC)
        eh_t = [turned[:, q] for q in range(2)]
        adj_t = adjt[:, :, :].bitcast(F16).rearrange("p b (t i) -> p b t i", i=P)
        raw = [adjt[:, :, :].bitcast(F16).rearrange("p b n -> p (b n)"), wide[:, 0:2 * NP]]
        mask_all = [m.bitcast(BF16) for m in raw]
        masks = [m.rearrange("p (u m i) -> p m u i", u=2, i=P) for m in mask_all]
        scores = [m[:, :, :].rearrange("p b n -> p (b n)").rearrange("p (m u i) -> p m u i", u=2, i=P)
                  for m in (chain, adjr)]
        ehl16 = ehl[:, :, :].bitcast(F16)
        num = ehl16.rearrange("p b (q t i) -> p b q t i", q=2, i=P)
        rows_t = ehl16.rearrange("p q (k n) -> p q k n", k=KC)
        chain_t = chain[:, :, :].rearrange("p b (t i) -> p b t i", i=P)
        run_max = slb[:, 0:BANK]
        wall = chain[:, 0, 0:KC * WCOLS].rearrange("p (k c) -> p k c", k=KC)
        arow = chain[:, 1, 0:2 * D].rearrange("p (q c) -> p q c", q=2)
        scrap = chain[:, 1, 2 * D:4 * D].rearrange("p (q c) -> p q c", q=2)
        smr = chain[0:6, 1, :]

        def col(n):
            return cvec[:, n:n + 1]
        srmin, nmx, nmx_all, gbias, zmax, zmax_all, zsum, zsum_all, zinv, l1scale, lnb, fac, lowest, zfac = map(col, range(14))

        adj_turned = nc.dram_tensor("adj_turned", [T, P, NP], F16, kind="Internal").ap()
        sl_row = nc.dram_tensor("sl_row", [1, NP], F32, kind="Internal").ap()

        tb = [ctx.enter_context(nc.psum_tensor(f"turn{k}", [P, BANK], F32)) for k in range(4)]
        acc_a = [ctx.enter_context(nc.psum_tensor(f"acc_a{b}", [P, BANK], F32)) for b in range(2)]
        acc_b = [ctx.enter_context(nc.psum_tensor(f"acc_b{b}", [P, BANK], F32)) for b in range(2)]
        sc_bank, mx_bank, bc_bank = tb, acc_a[0], acc_a[1]
        edge_bank = [[tb[2], tb[3]], [acc_a[0], acc_a[1]]]
        supp_bank = [acc_a[0], acc_b[0]]
        y_bank, v_bank = tb, acc_a + acc_b
        tb16 = [bank[:, :].bitcast(F16) for bank in tb]

        pad_zero = sem("pad_zero")
        x_loaded = [sem(f"x_loaded{n}") for n in range(len(X_PARTS))]
        cast_ok = sem("cast_ok")
        w_pow2 = sem("w_pow2")
        w_loaded, small_loaded, b_loaded = sem("w_loaded"), sem("small_loaded"), sem("b_loaded")
        adj_ready = [sem(f"adj_ready{b}") for b in range(2)]
        adj_pad = sem("adj_pad")
        ident_ok = sem("ident_ok")
        pool_sum = sem("pool_sum")
        u_ok = sem("u_ok")
        w_amax = sem("w_amax")
        w_scaled, w_hi, w_split = sem("w_scaled"), sem("w_hi"), sem("w_split")
        dve = sem("dve")
        fac_ok = sem("fac_ok")
        norm_ok = sem("norm_ok")
        hn_done = [sem(f"hn_done{b}") for b in range(RB)]
        hn_turned = sem("hn_turned")
        rows_hi = sem("rows_hi")
        rows_lo = sem("rows_lo")
        small_done = sem("small_done")
        nmx_ok = sem("nmx_ok")
        g_ok = sem("g_ok")
        cols_ok = sem("cols_ok")
        gcol_ok = sem("gcol_ok")
        small_mm, small_out = sem("small_mm"), sem("small_out")
        sl_stored = sem("sl_stored")
        slb_ok = sem("slb_ok")
        v_mm, v_hi_ok, v_lo_ok = sem("v_mm"), sem("v_hi_ok"), sem("v_lo_ok")
        y_mm, y_hi_ok, y_lo_ok = sem("y_mm"), sem("y_hi_ok"), sem("y_lo_ok")
        turn_mm = sem("turn_mm")
        turn_out = sem("turn_out")
        sum_ok = sem("sum_ok")
        relu_ok = sem("relu_ok")
        exp_ok = sem("exp_ok")
        mask_ok = sem("mask_ok")
        num_hi = sem("num_hi")
        num_lo = sem("num_lo")
        y_done = sem("y_done")
        v_done = sem("v_done")
        gate_in = sem("gate_in")
        gate_out = sem("gate_out")
        mix_in = sem("mix_in")
        mix_out = sem("mix_out")
        fin = sem("fin")
        st_ok = sem("st_ok")
        edge_mm = sem("edge_mm")
        edge_hi = sem("edge_hi")
        edge_lo = sem("edge_lo")
        supp_mm = sem("supp_mm")
        supp_hi = sem("supp_hi")
        supp_lo = sem("supp_lo")
        z_ok = sem("z_ok")
        zmax_in = sem("zmax_in")
        zneg_ok = sem("zneg_ok")
        zexp_ok = sem("zexp_ok")
        ones_ok = sem("ones_ok")
        adj_saved = [sem(f"adj_saved{b}") for b in range(2)]
        raw_loaded = [sem(f"raw_loaded{b}") for b in range(2)]
        mb_ok = sem("mb_ok")
        sc_mm = sem("sc_mm")
        scan_ok = sem("scan_ok")
        mx_ok = sem("mx_ok")
        mxt_mm = sem("mxt_mm")
        negm_ok = sem("negm_ok")
        bc_mm = sem("bc_mm")
        sub_ok = sem("sub_ok")
        expd = sem("expd")
        p_hi = sem("p_hi")
        p_lo, p_lo_last = sem("p_lo"), sem("p_lo_last")
        o_mm = sem("o_mm")
        fin1 = sem("fin1")
        keep_ok = sem("keep_ok")
        o_ok = sem("o_ok")
        stored = sem("stored")
        pool_mark = sem("pool_mark")

        adj_rows = adj[:, :]

        def split_product(pe, psum, parts_l, parts_r, start=True, stop=True):
            n = len(parts_l[0])
            for i, (a, c) in enumerate((a, c) for k in range(n) for a, c in
                                       ((parts_l[0][k], parts_r[0][k]), (parts_l[0][k], parts_r[1][k]),
                                        (parts_l[1][k], parts_r[0][k]))):
                mm = nc.tensor.matmul(psum, a, c, start=(i == 0), stop=(i == 3 * n - 1))
            return mm

        def carry(eng, mark):
            eng.sem_inc(mark, 1)

        block = ctx.enter_context(nc.Block())

        @block.sync
        def _(sp):
            body = (T - 1) * P
            for n, w in enumerate((W_sa, W_gcnb, edge_w, weight)):
                sp.dma_start(wall[:, :, n * D:(n + 1) * D], w.rearrange("(k p) c -> p k c", p=P)).then_inc(w_loaded, 16)
            for n, (t, m) in enumerate(X_PARTS):
                m = min(m, T - 1 - t)
                sp.dma_start(xres[:, t:t + m, :],
                             x[t * P:(t + m) * P, :].rearrange("(t p) d -> p t d", p=P)).then_inc(x_loaded[n], 16)
            sp.wait_ge(pad_zero, 1)
            sp.dma_start(xres[0:TAIL, T - 1, :], x[body:N, :]).then_inc(x_loaded[-1], 16)
            sp.wait_ge(small_loaded, 16 * SMALL_LOADS)

            def load(t, b, rows=P):
                sp.dma_start(adjr[0:rows, b, 0:N], adj_rows[bass.ds(t * P, rows), :]).then_inc(adj_ready[b], 16)

            def save(t, b):
                sp.wait_ge(turn_out, NG * (t + 1))
                sp.dma_start(adj_turned[bass.ds(t, 1), :, :].squeeze(),
                             adjt[:, b, :].bitcast(F16)).then_inc(adj_saved[b], 16)

            load(0, 0)
            load(1, 1)
            sp.wait_ge(cast_ok, 1)
            load(2, 0)
            sp.wait_ge(small_out, NCH)
            sp.dma_start(sl_row[:, :], smr[5:6, :]).then_inc(sl_stored, 16)
            sp.wait_ge(sl_stored, 16)
            sp.dma_start(slb[:, :], sl_row[0, :].partition_broadcast(P)).then_inc(slb_ok, 16)
            sp.wait_ge(cast_ok, 2)
            load(3, 1)
            with sp.Fori(0, T - 7, 2) as t0:
                for b in range(2):
                    save(t0 + b, b)
                    sp.wait_ge(cast_ok, t0 + b + 3)
                    load(t0 + b + 4, b)
            save(T - 6, 0)
            sp.wait_ge(cast_ok, T - 3)
            load(T - 2, 0)
            save(T - 5, 1)
            sp.wait_ge(cast_ok, T - 2)
            load(T - 1, 1, TAIL)
            for t in range(T - 4, T):
                save(t, t % 2)

            def load_raw(q, par):
                sp.dma_start(raw[par].rearrange("p (u n) -> p u n", u=2),
                             adj_turned[bass.ds(2 * q, 2), :, :].rearrange("u p n -> p u n")).then_inc(raw_loaded[par], 16)

            for b in range(2):
                sp.wait_ge(adj_saved[b], 8 * T)
            sp.wait_ge(y_done, T)
            sp.wait_ge(mask_ok, T)
            load_raw(0, 0)
            sp.wait_ge(edge_mm, KC * NCH)
            load_raw(1, 1)
            with sp.Fori(2, PAIRS - 2, 2) as q0:
                for par in range(2):
                    sp.wait_ge(scan_ok, PAIRS * (q0 + par - 1))
                    load_raw(q0 + par, par)
            sp.wait_ge(scan_ok, PAIRS * (PAIRS - 2))
            load_raw(PAIRS - 1, 0)

        @block.gpsimd
        def _(pool):
            nc.gpsimd.memset(ident[:, :], 0.0).then_inc(ident_ok, 1)
            nc.gpsimd.memset(adjr[:, :, N:NP], 0.0).then_inc(adj_pad, 1)
            pool.wait_ge(ident_ok, 1)
            nc.gpsimd.affine_select(out=ident[:, :], in_=ident[:, :], compare_op=ALU.not_equal, fill=1.0,
                                    base=0, pattern=[[-1, P]], channel_multiplier=1).then_inc(ident_ok, 1)
            pool.wait_ge(ident_ok, 2)
            nc.gpsimd.tensor_copy(ident16[:, :], ident[:, :]).then_inc(ident_ok, 1)
            pool.wait_ge(w_amax, len(GROUPS))
            nc.gpsimd.partition_all_reduce(amax_all[:, :], amax[:, :], P, bass.bass_isa.ReduceOp.max).then_inc(pool_sum, 1)
            pool.wait_ge(w_pow2, 1)
            for g, (c, w) in enumerate(GROUPS):
                nc.gpsimd.tensor_scalar(wall[:, :, c:c + w], wall[:, :, c:c + w], wscale[:, g:g + 1], 1.0,
                                        ALU.mult, ALU.mult).then_inc(w_scaled, 1)
            pool.wait_ge(w_scaled, len(GROUPS))
            for n, (c, w) in enumerate(SPLITS):
                nc.gpsimd.tensor_scalar(whi[:, :, c:c + w], wall[:, :, c:c + w], 1.0, 0.0, ALU.mult, ALU.add).then_inc(w_hi, 1)
                pool.wait_ge(w_hi, n + 1)
                nc.gpsimd.tensor_tensor(wlo[:, :, c:c + w], wall[:, :, c:c + w], whi[:, :, c:c + w],
                                        ALU.subtract).then_inc(w_split, 1)

            def cast(t, b, first=False):
                pool.wait_ge(adj_ready[b], 8 * (t - b) + 16)
                if not first:
                    pool.wait_ge(turn_mm, NG * t)
                carry(pool, pool_mark)
                nc.gpsimd.tensor_scalar(adj16[:, :], adjr[:, b, :], 1.0, 0.0, ALU.mult, ALU.add).then_inc(cast_ok, 1)

            pool.wait_ge(adj_pad, 1)
            cast(0, 0, True)
            pool.wait_ge(nmx_ok, 1)
            nc.gpsimd.partition_all_reduce(nmx_all, nmx, P, bass.bass_isa.ReduceOp.max).then_inc(pool_sum, 1)

            def low(t, b, first):
                pool.wait_ge(num_hi, t + 1)
                if not first:
                    pool.wait_ge(v_done, t - 1)
                nc.gpsimd.tensor_tensor(num[:, b, 1], chain_t[:, b], num[:, b, 0], ALU.subtract).then_inc(num_lo, 1)

            cast(1, 1)
            low(0, 0, True)
            cast(2, 0)
            low(1, 1, True)
            cast(3, 1)
            with pool.Fori(2, T - 3, 2) as t0:
                for b in range(2):
                    low(t0 + b, b, False)
                    cast(t0 + b + 2, b)
            low(T - 2, 0, False)
            low(T - 1, 1, False)

            def make_mask(par):
                pool.wait_ge(raw_loaded[par], 16)
                nc.gpsimd.tensor_scalar(mask_all[par], raw[par], MASKED, -MASKED, ALU.mult, ALU.add).then_inc(mb_ok, 1)

            make_mask(0)
            pool.wait_ge(z_ok, T)
            nc.gpsimd.affine_select(out=nodes[:, T - 1:T], in_=nodes[:, T - 1:T], compare_op=ALU.is_gt,
                                    fill=-MASKED, base=TAIL, pattern=[[0, 1]], channel_multiplier=-1).then_inc(pool_sum, 1)
            pool.wait_ge(zmax_in, 1)
            nc.gpsimd.partition_all_reduce(zmax_all, zmax, P, bass.bass_isa.ReduceOp.max).then_inc(pool_sum, 1)
            pool.wait_ge(zexp_ok, 1)
            nc.gpsimd.partition_all_reduce(zsum_all, zsum, P, bass.bass_isa.ReduceOp.add).then_inc(pool_sum, 1)

            def low(t, u, par):
                pool.wait_ge(expd, t + 1)
                nc.gpsimd.tensor_tensor(num[:, u, 1], scores[par][:, :, u, :], num[:, u, 0], ALU.subtract).then_inc(p_lo, 1)

            make_mask(1)
            for u in range(2):
                low(u, u, 0)
            with pool.Fori(1, PAIRS - 3, 2) as p0:
                for n in range(2):
                    for u in range(2):
                        low(2 * (p0 + n) + u, u, 1 - n)
            low(T - 4, 0, 1)
            low(T - 3, 1, 1)
            low(T - 2, 0, 0)

        @block.scalar
        def _(act):
            for q in range(2):
                act.dma_start(arow[:, q, :], a_sa[0, q * D:(q + 1) * D].partition_broadcast(P)).then_inc(w_loaded, 16)
            act.dma_start(wall[:, :, ND:ND + 1], node_w.rearrange("(k p) c -> p k c", p=P),
                          allow_slow_non_contiguous=True).then_inc(small_loaded, 16)
            for q in range(2):
                for n, g in enumerate((Wa, Wb)):
                    act.dma_start(wall[:, :, SM + 2 * q + n:SM + 2 * q + n + 1],
                                  g[0:1, q * D:(q + 1) * D].rearrange("o (k p) -> p k o", p=P),
                                  allow_slow_non_contiguous=True).then_inc(small_loaded, 16)
            act.dma_start(bg[:, :], b_gcnb.partition_broadcast(P)).then_inc(b_loaded, 16)
            act.dma_start(bw[:, :], bias.partition_broadcast(P)).then_inc(b_loaded, 16)
            act.dma_start(bab[:, 0:1], ba.partition_broadcast(P)).then_inc(b_loaded, 16)
            act.dma_start(bab[:, 1:2], bb.partition_broadcast(P)).then_inc(b_loaded, 16)

            def norm(layer, t, first=False):
                if not first:
                    act.wait_ge(hn_turned, T * layer + t - RB + 1)
                nc.scalar.activation(hn[layer][:, RB - 1, :], xres[:, bass.ds(t, 1), :].squeeze(), ACT.Identity,
                                     bias=shift[:, bass.ds(t, 1)], scale=rstd[:, bass.ds(t, 1)]).then_inc(hn_done[RB - 1], RB)

            def high(layer, t, b):
                act.wait_ge(hn_turned, T * layer + t + 1)
                nc.scalar.activation(rows_t[:, 0, :, bass.ds(t * P, P)],
                                     tb[b][:, 0:D].rearrange("p (k n) -> p k n", k=KC), ACT.Relu).then_inc(rows_hi, 1)

            def small_row(k, c, w):
                act.wait_ge(small_mm, k + 1)
                nc.scalar.activation(smr[:, bass.ds(c, w)], acc_a[0][0:6, 0:w], ACT.Copy, scale=fac[0:6]).then_inc(small_out, 1)

            act.wait_ge(norm_ok, 1)
            norm(0, RB - 1, True)
            for k in range(2):
                for n in range(BPB):
                    high(0, k * BPB + n, n)
                norm(0, (k + 2) * BPB - 1)
            act.wait_ge(fac_ok, 1)
            with act.Fori(2, NCH - 2) as k:
                small_row(k - 2, (k - 2) * BANK, BANK)
                for n in range(BPB):
                    high(0, k * BPB + n, n % RB)
                norm(0, (k + 2) * BPB - 1)
            small_row(NCH - 4, *CHUNKS[NCH - 4])
            for t in range((NCH - 2) * BPB, (NCH - 1) * BPB):
                high(0, t, t % RB)
            small_row(NCH - 3, *CHUNKS[NCH - 3])
            for t in range((NCH - 1) * BPB, T):
                high(0, t, t % RB)
            for k in range(NCH - 2, NCH):
                small_row(k, *CHUNKS[k])

            def y_high(t, b):
                act.wait_ge(y_mm, t + 1)
                nc.scalar.activation(y_hi[:, bass.ds(t, 1), 0:D].squeeze(), y_bank[b][:, 0:D], ACT.Copy,
                                     scale=OUT_SCALE).then_inc(y_hi_ok, 1)

            with act.Fori(0, T // RB * RB - RB + 1, RB) as t0:
                for b in range(RB):
                    y_high(t0 + b, b)
            for t in range(T // RB * RB, T):
                y_high(t, t % RB)
            act.wait_ge(g_ok, 1)
            nc.scalar.activation(gcol[:, :], sm[:, :, 4], ACT.Exp, bias=gbias, scale=-0.01).then_inc(gcol_ok, 1)
            nc.scalar.activation(eps_col[:, :], sm[:, :, 5], ACT.Exp, bias=gbias, scale=0.01).then_inc(gcol_ok, 1)

            act.wait_ge(gcol_ok, 3)
            def v_high(t, b):
                act.wait_ge(v_mm, t + 1)
                nc.scalar.activation(v_hi[:, bass.ds(t, 1), 0:D].squeeze(), v_bank[b][:, 0:D], ACT.Copy,
                                     scale=tmp_t[:, bass.ds(t, 1)]).then_inc(v_hi_ok, 1)

            def gate_tanh(t, b):
                act.wait_ge(gate_in, t + 1)
                nc.scalar.activation(tg[:, b, :], gates[:, b, :], ACT.Tanh, scale=0.5).then_inc(gate_out, 1)

            def mix_tanh(t, b):
                act.wait_ge(mix_in, t + 1)
                nc.scalar.activation(act_out[:, b, :], mix[:, b, :], ACT.Tanh, scale=0.5).then_inc(mix_out, 1)

            def expo(t, b):
                act.wait_ge(relu_ok, t + 1)
                nc.scalar.activation(chain[:, b, :], chain[:, b, :], ACT.Exp, scale=-0.99).then_inc(exp_ok, 1)

            def turned(t, b, g, early=False):
                act.wait_ge(turn_mm, NG * t + g + 1)
                if g == 0 and not early:
                    act.wait_ge(y_done, t - 1)
                    act.wait_ge(mask_ok, t - 1)
                    act.wait_ge(adj_saved[b], 8 * (t - b))
                m, n = GROUPS_T[g]
                nc.scalar.activation(adj_t[:, b, m:m + n].rearrange("p t i -> p (t i)"), tb16[g][:, 0:n * P],
                                     ACT.Copy).then_inc(turn_out, 1)

            def numer_high(t, b, early=False):
                act.wait_ge(mask_ok, t + 1)
                if not early:
                    act.wait_ge(v_done, t - 1)
                nc.scalar.activation(num[:, b, 0], chain_t[:, b], ACT.Copy).then_inc(num_hi, 1)

            for t in range(RB):
                v_high(t, t)
            for g in range(NG):
                turned(0, 0, g, True)
            def v_highs(start, end):
                with act.Fori(start, end - RB + 1, RB) as t0:
                    for b in range(RB):
                        v_high(t0 + b, b)

            v_highs(RB, T // RB * RB)
            for t in range(T // RB * RB, T):
                v_high(t, t % RB)
            expo(0, 0)
            for g in range(NG):
                turned(1, 1, g, True)
            numer_high(0, 0, True)
            expo(1, 1)
            numer_high(1, 1, True)
            with act.Fori(2, T - 1, 2) as t0:
                for b in range(2):
                    t = t0 + b
                    gate_tanh(t - 2, b)
                    expo(t, b)
                    turned(t, b, 0)
                    turned(t, b, 1)
                    mix_tanh(t - 2, b)
                    turned(t, b, 2)
                    turned(t, b, 3)
                    numer_high(t, b)
            act.wait_ge(norm_ok, 2)
            norm(1, RB - 1, True)
            gate_tanh(T - 2, 0)
            mix_tanh(T - 2, 0)
            act.wait_ge(v_done, T - 1)
            for t in range(RB):
                high(1, t, t)
            norm(1, 2 * RB - 1)

            def support_high(t, b):
                act.wait_ge(supp_mm, t + 1)
                nc.scalar.activation(nodes[:, bass.ds(t, 1)], supp_bank[b][:, D:D + 1], ACT.Copy, scale=zfac).then_inc(z_ok, 1)
                nc.scalar.activation(s_hi[:, bass.ds(t, 1), 0:D].squeeze(), supp_bank[b][:, 0:D], ACT.Copy,
                                     scale=OUT_SCALE).then_inc(supp_hi, 1)

            gate_tanh(T - 1, 1)
            high(1, RB, 0)
            high(1, RB + 1, 1)
            support_high(0, 0)
            mix_tanh(T - 1, 1)
            high(1, RB + 2, 2)
            support_high(1, 1)
            high(1, RB + 3, 3)
            norm(1, 3 * RB - 1)
            support_high(2, 0)
            support_high(3, 1)
            with act.Fori(2 * RB, LOOPED - RB + 1, RB) as t0:
                for b in range(RB):
                    high(1, t0 + b, b)
                    support_high(t0 + b - SUP, (b - SUP) % 2)
                norm(1, t0 + 2 * RB - 1)
            for t in range(LOOPED, T // RB * RB):
                high(1, t, t % RB)
                support_high(t - SUP, (t - SUP) % 2)
            for t in range(T // RB * RB, T + SUP):
                if t < T:
                    high(1, t, t % RB)
                support_high(t - SUP, (t - SUP) % 2)

            def edge_high(k, c, w, par):
                for m in range(KC):
                    act.wait_ge(edge_mm, KC * k + m + 1)
                    nc.scalar.activation(eh_t[0][:, m, bass.ds(c, w)], edge_bank[par][m][:, 0:w], ACT.Copy,
                                         scale=OUT_SCALE).then_inc(edge_hi, 1)
            with act.Fori(0, NCH - 2, 2) as k0:
                for par in range(2):
                    edge_high(k0 + par, (k0 + par) * BANK, BANK, par)
            edge_high(NCH - 1, *CHUNKS[-1], 0)
            act.wait_ge(zneg_ok, 1)
            nc.scalar.activation(nodes[:, :], nodes[:, :], ACT.Exp, bias=zmax_all, accum_out=zsum).then_inc(zexp_ok, 1)

            def make_mask(q, par):
                act.wait_ge(raw_loaded[par], 8 * (q - par) + 16)
                nc.scalar.activation(mask_all[par], raw[par], ACT.Identity, bias=lowest, scale=MASKED).then_inc(mb_ok, 1)

            def numer(t, u, par, first=False):
                act.wait_ge(sub_ok, t + 1)
                if not first:
                    act.wait_ge(o_mm, t - 1)
                nc.scalar.activation(num[:, u, 0], scores[par][:, :, u, :], ACT.Exp, bias=lnb,
                                     scale=l1scale).then_inc(p_hi, 1)
                act.wait_ge(p_hi, t + 1)
                nc.scalar.activation(scores[par][:, :, u, :], scores[par][:, :, u, :], ACT.Exp, bias=lnb,
                                     scale=l1scale).then_inc(expd, 1)

            def store(t):
                act.wait_ge(o_ok, t + 1)
                act.dma_start(out[bass.ds(t * P, P), :], xres[:, bass.ds(t, 1), :].squeeze()).then_inc(stored, 16)

            def pair(p, par, first=False, masks_left=True):
                numer(2 * p, 0, par, first)
                if masks_left:
                    make_mask(p + 2, par)
                if not first:
                    store(2 * p - 2)
                numer(2 * p + 1, 1, par, first)
                if not first:
                    store(2 * p - 1)

            pair(0, 0, first=True)
            with act.Fori(1, PAIRS - 3, 2) as p0:
                for n in range(2):
                    pair(p0 + n, 1 - n)
            pair(PAIRS - 2, 1, masks_left=False)
            pair(PAIRS - 1, 0, masks_left=False)
            store(T - 2)
            act.wait_ge(o_ok, T)
            act.dma_start(out[(T - 1) * P:N, :], xres[0:TAIL, T - 1, :]).then_inc(stored, 16)
            act.wait_ge(stored, 16 * T)

        @block.vector
        def _(vec):
            count = [0]

            def step(ins):
                count[0] += 1
                ins.then_inc(dve, 1)
                vec.wait_ge(dve, count[0])

            def free(ins):
                count[0] += 1
                ins.then_inc(dve, 1)

            v = nc.vector
            v.memset(xres[96:P, T - 1, :], 0.0).then_inc(pad_zero, 1)
            step(v.memset(lnb, LN_EXP_SCALE))
            step(v.memset(lowest, -MASKED))
            step(v.memset(wall[:, :, WCOLS - 1:WCOLS], 0.0))

            def x_stats(n):
                t, m = X_PARTS[n]
                vec.wait_ge(x_loaded[n], 16 if n + 1 < len(X_PARTS) else 32)
                for b in range(m):
                    v.bn_stats(stats[:, t + b, :], xres[:, t + b, :]).then_inc(st_ok, 1)

            def biggest_weight(g):
                c, w = GROUPS[g]
                v.tensor_reduce(amax[:, g:g + 1], wall[:, :, c:c + w], XY, ALU.max,
                                apply_absolute_value=True).then_inc(w_amax, 1)

            vec.wait_ge(w_loaded, 16 * W_LOADS)
            for k in range(KC):
                for q, c in ((1, U_R), (0, U_L)):
                    v.tensor_tensor_reduce(out=scrap[:, q], in0=wall[:, k, SA:SA + D], in1=arow[:, q, :], scale=1.0,
                                           scalar=0.0, op0=ALU.mult, op1=ALU.add, accum_out=wall[:, k, c:c + 1]).then_inc(u_ok, 1)
                vec.wait_ge(u_ok, 2 * (k + 1))
            for g in (G_SA, G_GC, G_ED, G_WT):
                biggest_weight(g)
            x_stats(0)
            x_stats(1)
            vec.wait_ge(small_loaded, 16 * SMALL_LOADS)
            for g in (G_ND, G_SM):
                biggest_weight(g)
            x_stats(2)
            x_stats(3)

            def norm_steps(a, z):
                st = stats[:, a:z, :]
                me, te, va, rs, sh = (m[:, a:z] for m in (mean, tmp_n, var, rstd, shift))
                free(v.tensor_tensor(me, st[:, :, 1], st[:, :, 4], ALU.add))
                free(v.tensor_tensor(va, st[:, :, 2], st[:, :, 5], ALU.add))
                step(v.tensor_tensor(te, st[:, :, 1], st[:, :, 4], ALU.subtract))
                yield
                free(v.tensor_scalar(va, va, 1.0 / D, EPS_LN, ALU.mult, ALU.add))
                step(v.scalar_tensor_tensor(out=te, in0=te, scalar=0.25, in1=te, op0=ALU.mult, op1=ALU.mult))
                step(v.tensor_tensor(va, va, te, ALU.add))
                yield
                step(v.tensor_scalar(rs.bitcast(I32), va.bitcast(I32), -0.5, RSQRT_BITS, ALU.mult, ALU.add))
                for scale in (1.0, 1.0, H_SCALE):
                    step(v.scalar_tensor_tensor(out=te, in0=rs, scalar=-0.5 * scale, in1=rs, op0=ALU.mult, op1=ALU.mult))
                    yield
                    step(v.tensor_tensor(te, te, va, ALU.mult))
                    step(v.scalar_tensor_tensor(out=rs, in0=te, scalar=1.5 * scale, in1=rs, op0=ALU.add, op1=ALU.mult))
                    yield
                step(v.scalar_tensor_tensor(out=sh, in0=me, scalar=-0.5, in1=rs, op0=ALU.mult, op1=ALU.mult))

            def norm_stats(a, z):
                for _ in norm_steps(a, z):
                    pass
                v.nop().then_inc(norm_ok, 1)

            def norm(layer, t, b, first=False):
                if not first:
                    vec.wait_ge(hn_turned, T * layer + t - RB + 1)
                v.tensor_scalar(hn[layer][:, b, :], xres[:, bass.ds(t, 1), :].squeeze(), rstd[:, bass.ds(t, 1)],
                                shift[:, bass.ds(t, 1)], ALU.mult, ALU.add).then_inc(hn_done[b], RB)

            def rows_low(layer, t, b):
                vec.wait_ge(rows_hi, T * layer + t + 1)
                v.scalar_tensor_tensor(out=rows_t[:, 1, :, bass.ds(t * P, P)],
                                       in0=tb[b][:, 0:D].rearrange("p (k n) -> p k n", k=KC), scalar=0.0,
                                       in1=rows_t[:, 0, :, bass.ds(t * P, P)], op0=ALU.max,
                                       op1=ALU.subtract).then_inc(rows_lo, 1)

            vec.wait_ge(st_ok, T)
            norm_stats(0, T)
            for t in range(RB - 1):
                norm(0, t, t, True)

            vec.wait_ge(pool_sum, 1)
            step(v.tensor_scalar(amax_all[:, :], amax_all[:, :], 1e-30, None, ALU.max))
            step(v.tensor_scalar(pow2[:, :].bitcast(U32), amax_all[:, :].bitcast(U32), 0x7F800000, None, ALU.bitwise_and))
            step(v.reciprocal(wscale[:, :], pow2[:, :]))
            step(v.tensor_scalar(wscale[:, :], wscale[:, :], W_TOP, None, ALU.mult))
            v.nop().then_inc(w_pow2, 1)
            step(v.tensor_scalar(unsc[:, :], pow2[:, :], UNSCALE, None, ALU.mult))
            step(v.tensor_tensor(l1scale, unsc[:, G_ED:G_ED + 1], unsc[:, G_ED:G_ED + 1], ALU.mult))
            step(v.tensor_scalar(fac, unsc[:, G_SM:G_SM + 1], OUT_SCALE, None, ALU.mult))
            step(v.tensor_scalar(zfac, unsc[:, G_ND:G_ND + 1], OUT_SCALE, None, ALU.mult))
            v.nop().then_inc(fac_ok, 1)

            with vec.Fori(0, LOOPED - RB + 1, RB) as t0:
                for b in range(RB):
                    rows_low(0, t0 + b, b)
                    if b < RB - 1:
                        norm(0, t0 + b + RB, b)
            for t in range(LOOPED, T):
                rows_low(0, t, t % RB)
                if t + RB < T:
                    norm(0, t + RB, t % RB)

            def y_low(t, b):
                vec.wait_ge(y_hi_ok, t + 1)
                v.scalar_tensor_tensor(out=y_lo[:, bass.ds(t, 1), 0:D].squeeze(), in0=y_bank[b][:, 0:D],
                                       scalar=OUT_SCALE, in1=y_hi[:, bass.ds(t, 1), 0:D].squeeze(),
                                       op0=ALU.mult, op1=ALU.subtract).then_inc(y_lo_ok, 1)

            for t in range(RB):
                y_low(t, t)
            vec.wait_ge(small_done, 1)
            step(v.tensor_copy(sm[:, :, :], acc_b[0][:, 0:8 * T].rearrange("p (t c) -> p t c", c=8)[:, :, 0:6]))
            step(v.tensor_reduce(srmin, sm[:, :, 4], X, ALU.min))
            step(v.tensor_scalar(nmx, srmin, -1.0, None, ALU.mult))
            v.nop().then_inc(nmx_ok, 1)

            with vec.Fori(RB, T // RB * RB - RB + 1, RB) as t0:
                for b in range(RB):
                    y_low(t0 + b, b)
            for t in range(T // RB * RB, T):
                y_low(t, t % RB)
            vec.wait_ge(pool_sum, 2)
            step(v.tensor_scalar(gbias, nmx_all, -0.01, None, ALU.mult))
            v.nop().then_inc(g_ok, 1)
            vec.wait_ge(gcol_ok, 2)
            step(v.tensor_scalar(tmp_t[:, :], gcol[:, :], OUT_SCALE, None, ALU.mult))
            v.nop().then_inc(gcol_ok, 1)

            def sums(t, b, m=0, n=T):
                ins = v.tensor_tensor(chain_t[:, b, m:m + n], slb[:, bass.ds(t * P, P)].unsqueeze(1).broadcast_to([P, n, P]),
                                      srt[:, m:m + n].unsqueeze(2).broadcast_to([P, n, P]), ALU.add)
                if m + n == T:
                    ins.then_inc(sum_ok, 1)

            def relu(t, b):
                vec.wait_ge(sum_ok, t + 1)
                v.tensor_scalar(chain[:, b, :], chain[:, b, :], 0.0, None, ALU.max).then_inc(relu_ok, 1)

            def v_low(t, b):
                vec.wait_ge(v_hi_ok, t + 1)
                v.scalar_tensor_tensor(out=v_lo[:, bass.ds(t, 1), 0:D].squeeze(), in0=v_bank[b][:, 0:D],
                                       scalar=tmp_t[:, bass.ds(t, 1)], in1=v_hi[:, bass.ds(t, 1), 0:D].squeeze(),
                                       op0=ALU.mult, op1=ALU.subtract).then_inc(v_lo_ok, 1)

            def v_lows(start, end):
                with vec.Fori(start, end - RB + 1, RB) as t0:
                    for b in range(RB):
                        v_low(t0 + b, b)

            v_lows(0, 2 * RB)
            step(v.tensor_copy(srt[:, :], sm[:, :, 4]))
            step(v.tensor_scalar(sm[:, :, 0:2], sm[:, :, 0:2], wscale[:, G_SM:G_SM + 1], None, ALU.mult))
            step(v.tensor_copy(y_hi[:, :, D:D + 2], sm[:, :, 0:2]))
            step(v.tensor_tensor(y_lo[:, :, D:D + 2], sm[:, :, 0:2], y_hi[:, :, D:D + 2], ALU.subtract))
            v.nop().then_inc(cols_ok, 1)
            v_lows(2 * RB, 3 * RB)
            vec.wait_ge(slb_ok, 16)
            vec.wait_ge(w_split, len(SPLITS))
            sums(0, 0, 0, T // 2)
            v_lows(3 * RB, 4 * RB)
            sums(0, 0, T // 2, T // 2)
            v_lows(4 * RB, 5 * RB)
            relu(0, 0)
            v_lows(5 * RB, T // RB * RB)
            for t in range(T // RB * RB, T):
                v_low(t, t % RB)

            FIN = 9

            def finish_a(t, b):
                vec.wait_ge(v_done, t + 1)
                v.scalar_tensor_tensor(out=gates[:, b, :], in0=acc_a[b][:, D:D + 2], scalar=unsc[:, G_SM:G_SM + 1],
                                       in1=rab[:, bass.ds(t, 1), :].squeeze(), op0=ALU.mult, op1=ALU.add).then_inc(gate_in, 1)
                v.tensor_scalar(den[:, b, 0:1], acc_b[b][:, D:D + 1], eps_col[:, bass.ds(t, 1)], None,
                                ALU.add).then_inc(fin, 1)
                v.scalar_tensor_tensor(out=mix[:, b, :], in0=acc_a[b][:, 0:D], scalar=unsc[:, G_GC:G_GC + 1],
                                       in1=bg[:, :], op0=ALU.mult, op1=ALU.add).then_inc(fin, 1)
                vec.wait_ge(fin, FIN * t + 1)
                v.reciprocal(den[:, b, 1:2], den[:, b, 0:1]).then_inc(fin, 1)

            def finish_b(t, b):
                vec.wait_ge(gate_out, t + 1)
                v.tensor_scalar(tg[:, b, :], tg[:, b, :], 0.5, 0.5, ALU.mult, ALU.add).then_inc(fin, 1)
                vec.wait_ge(fin, FIN * t + 4)
                v.tensor_scalar(den[:, b, 2:3], tg[:, b, 0:1], den[:, b, 1:2], fac, ALU.mult, ALU.mult).then_inc(fin, 1)
                v.tensor_scalar(mix[:, b, :], mix[:, b, :], tg[:, b, 1:2], None, ALU.mult).then_inc(fin, 1)
                vec.wait_ge(fin, FIN * t + 6)
                v.scalar_tensor_tensor(out=mix[:, b, :], in0=acc_b[b][:, 0:D], scalar=den[:, b, 2:3],
                                       in1=mix[:, b, :], op0=ALU.mult, op1=ALU.add).then_inc(mix_in, 1)

            def finish_c(t, b):
                vec.wait_ge(mix_out, t + 1)
                v.tensor_scalar(act_out[:, b, :], act_out[:, b, :], 0.5, 0.5, ALU.mult, ALU.add).then_inc(fin, 1)
                vec.wait_ge(fin, FIN * t + 7)
                xt = xres[:, bass.ds(t, 1), :].squeeze()
                v.tensor_tensor(xt, act_out[:, b, :], xt, ALU.add).then_inc(fin, 1)
                vec.wait_ge(fin, FIN * t + 8)
                v.bn_stats(stats[:, bass.ds(t, 1), :].squeeze(), xt).then_inc(fin, 1)

            def attend(t, b, early=False):
                if not early:
                    vec.wait_ge(num_lo, t - 1)
                if not (early and b == 0):
                    sums(t, b)
                    relu(t, b)
                if not early:
                    finish_a(t - 2, b)
                    finish_b(t - 2, b)
                    finish_c(t - 2, b)
                if early and b == 0:
                    columns()
                vec.wait_ge(exp_ok, t + 1)
                vec.wait_ge(turn_out, NG * (t + 1))
                v.tensor_tensor(chain_t[:, b], chain_t[:, b], adj_t[:, b], ALU.mult).then_inc(mask_ok, 1)

            def columns():
                step(v.tensor_scalar(gcol[:, :], gcol[:, :], G_SCALE, None, ALU.mult))
                step(v.tensor_copy(v_hi[:, :, D], gcol[:, :]))
                step(v.tensor_tensor(v_lo[:, :, D], gcol[:, :], v_hi[:, :, D], ALU.subtract))
                v.nop().then_inc(cols_ok, 1)

            attend(0, 0, True)
            vec.wait_ge(b_loaded, 16 * 4)
            for n in range(2):
                step(v.tensor_scalar(rab[:, :, n], sm[:, :, 2 + n], bab[:, n:n + 1], None, ALU.add))
            step(v.tensor_scalar(eps_col[:, :], eps_col[:, :], EPS_ATT * G_SCALE, None, ALU.mult))
            step(v.tensor_scalar(fac, unsc[:, G_SA:G_SA + 1], G_SCALE, None, ALU.mult))
            attend(1, 1, True)
            with vec.Fori(2, T - 1, 2) as t0:
                for b in range(2):
                    attend(t0 + b, b)
            vec.wait_ge(fin, FIN * (T - 2))
            norm_stats(0, T - 2)
            for t in range(RB - 1):
                norm(1, t, t, True)
            finish_a(T - 2, 0)
            finish_b(T - 2, 0)
            finish_c(T - 2, 0)
            for t in range(RB, 2 * RB - 1):
                norm(1, t, t % RB)
            vec.wait_ge(v_done, T)
            for t in range(RB):
                rows_low(1, t, t)

            def support_low(t, b):
                vec.wait_ge(supp_hi, t + 1)
                v.scalar_tensor_tensor(out=s_lo[:, bass.ds(t, 1), 0:D].squeeze(), in0=supp_bank[b][:, 0:D],
                                       scalar=OUT_SCALE, in1=s_hi[:, bass.ds(t, 1), 0:D].squeeze(),
                                       op0=ALU.mult, op1=ALU.subtract).then_inc(supp_lo, 1)

            finish_a(T - 1, 1)
            rows_low(1, RB, 0)
            norm(1, 2 * RB, 0)
            finish_b(T - 1, 1)
            rows_low(1, RB + 1, 1)
            norm(1, 2 * RB + 1, 1)
            finish_c(T - 1, 1)
            support_low(0, 0)
            rows_low(1, RB + 2, 2)
            norm(1, 2 * RB + 2, 2)
            support_low(1, 1)
            rows_low(1, RB + 3, 3)
            support_low(2, 0)
            support_low(3, 1)
            v.memset(s_hi[:, :, D:CV], 1.0).then_inc(ones_ok, 1)
            v.memset(s_lo[:, :, D:CV], 0.0).then_inc(ones_ok, 1)

            def rows_and_support(start, end):
                with vec.Fori(start, end - RB + 1, RB) as t0:
                    for b in range(RB):
                        rows_low(1, t0 + b, b)
                        if b < RB - 1:
                            norm(1, t0 + b + RB, b)
                        support_low(t0 + b - SUP, (b - SUP) % 2)

            vec.wait_ge(fin, FIN * T)
            steps = norm_steps(T - 2, T)
            for t in range(2 * RB, 4 * RB):
                rows_low(1, t, t % RB)
                if t % RB < RB - 1:
                    norm(1, t + RB, t % RB)
                next(steps, None)
                support_low(t - SUP, (t - SUP) % 2)
            for _ in steps:
                pass
            rows_and_support(4 * RB, LOOPED)
            for t in range(LOOPED, T + SUP):
                if t < T:
                    rows_low(1, t, t % RB)
                if t + RB < T:
                    norm(1, t + RB, t % RB)
                support_low(t - SUP, (t - SUP) % 2)

            def edge_low(k, c, w, par):
                for m in range(KC):
                    vec.wait_ge(edge_hi, KC * k + m + 1)
                    v.scalar_tensor_tensor(out=eh_t[1][:, m, bass.ds(c, w)], in0=edge_bank[par][m][:, 0:w],
                                           scalar=OUT_SCALE, in1=eh_t[0][:, m, bass.ds(c, w)], op0=ALU.mult,
                                           op1=ALU.subtract).then_inc(edge_lo, 1)
            with vec.Fori(0, NCH - 2, 2) as k0:
                for par in range(2):
                    edge_low(k0 + par, (k0 + par) * BANK, BANK, par)
            edge_low(NCH - 1, *CHUNKS[-1], 0)
            vec.wait_ge(pool_sum, 3)
            step(v.tensor_reduce(zmax, nodes[:, :], X, ALU.max))
            v.nop().then_inc(zmax_in, 1)
            vec.wait_ge(pool_sum, 4)
            step(v.tensor_scalar(zmax_all, zmax_all, -1.0, None, ALU.mult))
            v.nop().then_inc(zneg_ok, 1)
            vec.wait_ge(pool_sum, 5)
            step(v.reciprocal(zinv, zsum_all))
            step(v.tensor_scalar(nodes[:, :], nodes[:, :], zinv, unsc[:, G_WT:G_WT + 1], ALU.mult, ALU.mult))

            F1 = 3

            def scan(p, par, c, first=False):
                if c == 0:
                    vec.wait_ge(mb_ok, p + 1)
                    if not first:
                        vec.wait_ge(p_lo, 2 * p - 2)
                vec.wait_ge(sc_mm, PAIRS * p + c + 1)
                v.tensor_tensor(scores[par][:, 2 * c:2 * c + 2],
                                sc_bank[c % SB][:, :].rearrange("p (m u i) -> p m u i", u=2, i=P),
                                masks[par][:, 2 * c:2 * c + 2], ALU.add).then_inc(scan_ok, 1)

            def top(p, par):
                vec.wait_ge(mxt_mm, p + 1)
                v.tensor_reduce(negm[:, par, :], mx_bank[:, :].rearrange("p (u n) -> p u n", u=2), X, ALU.max,
                                negate=True).then_inc(negm_ok, 1)

            def off(p, par, u):
                vec.wait_ge(bc_mm, p + 1)
                v.tensor_tensor(scores[par][:, :, u, :], scores[par][:, :, u, :],
                                bc_bank[:, u * P:(u + 1) * P].unsqueeze(1).broadcast_to([P, T, P]), ALU.add).then_inc(sub_ok, 1)

            def biggest(p, par, c, first=False):
                vec.wait_ge(scan_ok, PAIRS * p + c + 1)
                if c > 1:
                    vec.wait_ge(mx_ok, (PAIRS - 1) * p + c - 1)
                elif not first:
                    vec.wait_ge(mxt_mm, p)
                chunk = [scores[par][:, 2 * n:2 * n + 2].rearrange("p m u i -> p (m u i)") for n in (0, c)]
                v.tensor_tensor(run_max, chunk[0] if c == 1 else run_max, chunk[1], ALU.max).then_inc(mx_ok, 1)

            def keep(par, u):
                v.tensor_scalar(den[:, u, 3:4], negm[:, par, u:u + 1], 0.5 * MASKED, None, ALU.is_lt).then_inc(keep_ok, 1)

            def finish(t, b):
                vec.wait_ge(o_mm, t + 1)
                v.reciprocal(den[:, b, 0:1], acc_b[b][:, D:D + 1]).then_inc(fin1, 1)
                vec.wait_ge(fin1, F1 * t + 1)
                vec.wait_ge(keep_ok, t + 1)
                v.tensor_scalar(den[:, b, 1:2], den[:, b, 0:1], nodes[:, bass.ds(t, 1)], den[:, b, 3:4],
                                ALU.mult, ALU.mult).then_inc(fin1, 1)
                vec.wait_ge(fin1, F1 * t + 2)
                xt = xres[:, bass.ds(t, 1), :].squeeze()
                v.scalar_tensor_tensor(out=mix[:, b, :], in0=acc_b[b][:, 0:D], scalar=den[:, b, 1:2], in1=xt,
                                       op0=ALU.mult, op1=ALU.add).then_inc(fin1, 1)
                vec.wait_ge(fin1, F1 * t + 3)
                v.tensor_tensor(xt, mix[:, b, :], bw[:, :], ALU.add).then_inc(o_ok, 1)

            def pair(p, par, first=False, last=False):
                for c in range(PAIRS):
                    if not last:
                        scan(p + 1, 1 - par, c, first)
                        if c > 1:
                            biggest(p + 1, 1 - par, c - 1)
                    if c == 0:
                        top(p, par)
                        vec.wait_ge(negm_ok, p + 1)
                    if c == 1:
                        if not first:
                            finish(2 * p - 2, 0)
                        keep(par, 0)
                        off(p, par, 0)
                    if c == 4:
                        off(p, par, 1)
                    if c == 8:
                        if not first:
                            finish(2 * p - 1, 1)
                        keep(par, 1)
                if not last:
                    biggest(p + 1, 1 - par, PAIRS - 1)

            for c in range(PAIRS):
                scan(0, 0, c, True)
                if c > 0:
                    biggest(0, 0, c, True)
            pair(0, 0, first=True)
            with vec.Fori(1, PAIRS - 3, 2) as p0:
                for n in range(2):
                    pair(p0 + n, 1 - n)
            pair(PAIRS - 2, 1)
            pair(PAIRS - 1, 0, last=True)
            vec.wait_ge(expd, T)
            v.tensor_tensor(num[:, 1, 1], scores[0][:, :, 1, :], num[:, 1, 0], ALU.subtract).then_inc(p_lo_last, 1)
            finish(T - 2, 0)
            finish(T - 1, 1)

        @block.tensor
        def _(pe):
            pe.wait_ge(ident_ok, 3)

            def lhs(t):
                return [[rows_t[:, q, k, bass.ds(t * P, P)] for k in range(KC)] for q in range(2)]

            def wcols(c, w):
                return [[m[:, k, c:c + w] for k in range(KC)] for m in (whi, wlo)]

            def row_turn(layer, t, b, first=False):
                pe.wait_ge(hn_done[b], RB * len(range(b, T, RB)) * layer + t - b + RB)
                if not first:
                    pe.wait_ge(rows_lo, T * layer + t - RB + 1)
                for k in range(KC):
                    tr = nc.tensor.transpose(tb[b][:, k * P:(k + 1) * P], hn[layer][:, b, k * P:(k + 1) * P], ident[:, :])
                tr.then_inc(hn_turned, 1)

            def small_rows(k, c, w, first=False):
                pe.wait_ge(rows_lo, k * BPB + min(BPB, w // P))
                if not first:
                    pe.wait_ge(small_out, k)
                split_product(pe, acc_a[0][0:6, 0:w], wcols(SM, 6),
                              [[rows_t[:, q, j, bass.ds(c, w)] for j in range(KC)] for q in range(2)]).then_inc(small_mm, 1)

            for t in range(BPB):
                row_turn(0, t, t % RB, t < RB)
            for n in range(BPB):
                row_turn(0, BPB + n, n % RB)
            pe.wait_ge(w_split, 1)
            small_rows(0, *CHUNKS[0], True)
            with pe.Fori(2, NCH - 1) as k:
                for n in range(BPB):
                    row_turn(0, k * BPB + n, n % RB)
                small_rows(k - 1, (k - 1) * BANK, BANK)
            for t in range((NCH - 1) * BPB, T):
                row_turn(0, t, t % RB)
            small_rows(NCH - 2, *CHUNKS[-2])
            small_rows(NCH - 1, *CHUNKS[-1])

            def project(t, bank, c, done, read, first=False):
                if not first:
                    pe.wait_ge(read, t - RB + 1)
                split_product(pe, bank[:, 0:D], lhs(t), wcols(c, D)).then_inc(done, 1)

            def project_rest(banks, c, done, read):
                with pe.Fori(RB, T // RB * RB - RB + 1, RB) as t0:
                    for b in range(RB):
                        project(t0 + b, banks[b], c, done, read)
                for t in range(T // RB * RB, T):
                    project(t, banks[t % RB], c, done, read)

            pe.wait_ge(w_split, 2)
            for t in range(RB):
                project(t, y_bank[t], GC, y_mm, y_lo_ok, True)
            pe.wait_ge(small_out, NCH)
            for t in range(T):
                tr = nc.tensor.transpose(acc_b[0][:, t * 8:t * 8 + 6], smr[:, t * P:(t + 1) * P], ident[0:6, 0:6])
            tr.then_inc(small_done, 1)
            project_rest(y_bank, GC, y_mm, y_lo_ok)

            def turn(t, g, first=False):
                if g == 0:
                    pe.wait_ge(cast_ok, t + 1)
                if not first:
                    pe.wait_ge(turn_out, NG * (t - 1) + g + 1)
                m, n = GROUPS_T[g]
                for j in range(n):
                    tr = nc.tensor.transpose(tb16[g][:, j * P:(j + 1) * P], adj16[:, (m + j) * P:(m + j + 1) * P],
                                             ident16[:, :])
                tr.then_inc(turn_mm, 1)

            def gather(t, b, g):
                pe.wait_ge(turn_out, NG * t + g + 1)
                m0, n = GROUPS_T[g]
                for m in range(m0, m0 + n):
                    for q, y in enumerate((y_hi, y_lo)):
                        mm = nc.tensor.matmul(acc_a[b][:, 0:CV], adj_t[:, b, m], y[:, m, :],
                                              start=(m == 0 and q == 0), stop=(m == T - 1 and q == 1))
                if g == NG - 1:
                    mm.then_inc(y_done, 1)

            def attend(t, b, last=False):
                pe.wait_ge(num_hi, t + 1)
                for m in range(T):
                    for q, y in enumerate((v_hi, v_lo)):
                        nc.tensor.matmul(acc_b[b][:, 0:D + 1], num[:, b, 0, m], y[:, m, 0:D + 1],
                                         start=(m == 0 and q == 0), stop=False)
                if last:
                    for n in range(RB):
                        row_turn(1, n, n, True)
                pe.wait_ge(num_lo, t + 1)
                for m in range(T):
                    mm = nc.tensor.matmul(acc_b[b][:, 0:D + 1], num[:, b, 1, m], v_hi[:, m, 0:D + 1],
                                          start=False, stop=(m == T - 1))
                mm.then_inc(v_done, 1)

            def tile0(t, b, last=False):
                pe.wait_ge(mix_in, t - 1)
                for g in range(NG):
                    if not last:
                        turn(t + 1, g)
                    gather(t, b, g)
                attend(t, b, last)

            pe.wait_ge(w_split, 3)
            for t in range(RB):
                project(t, v_bank[t], SA, v_mm, v_lo_ok, True)
            pe.wait_ge(y_lo_ok, T)
            for g in range(NG):
                turn(0, g, first=True)
            project_rest(v_bank, SA, v_mm, v_lo_ok)
            for g in range(NG):
                turn(1, g)
            pe.wait_ge(cols_ok, 1)
            pe.wait_ge(v_lo_ok, T)
            for b in range(2):
                for g in range(NG):
                    gather(b, b, g)
            pe.wait_ge(cols_ok, 2)
            attend(0, 0)
            for g in range(NG):
                turn(2, g)
            attend(1, 1)
            with pe.Fori(2, T - 3, 2) as t0:
                for b in range(2):
                    tile0(t0 + b, b)
            tile0(T - 2, 0)
            tile0(T - 1, 1, last=True)

            def support(t, b, first=False):
                pe.wait_ge(rows_lo, T + t + 1)
                if not first:
                    pe.wait_ge(supp_lo, t - 1)
                split_product(pe, supp_bank[b][:, 0:D + 1], lhs(t), wcols(WT, D + 1)).then_inc(supp_mm, 1)

            for t in range(RB, 2 * RB):
                row_turn(1, t, t % RB)
            pe.wait_ge(w_split, len(SPLITS))
            pe.wait_ge(mix_in, T - 1)
            for t in range(RB):
                support(t, t % 2, t < 2)
            with pe.Fori(2 * RB, T // RB * RB - RB + 1, RB) as t0:
                for b in range(RB):
                    row_turn(1, t0 + b, b)
                    support(t0 + b - RB, b % 2)
            for t in range(T // RB * RB, T + RB):
                if t < T:
                    row_turn(1, t, t % RB)
                support(t - RB, t % 2)

            def edge(k, c, w, par, first=False):
                for m in range(KC):
                    if not first:
                        pe.wait_ge(edge_lo, KC * (k - 2) + m + 1)
                    split_product(pe, edge_bank[par][m][:, 0:w], wcols(ED + m * P, P),
                                  [[rows_t[:, q, j, bass.ds(c, w)] for j in range(KC)] for q in range(2)]).then_inc(edge_mm, 1)

            edge(0, 0, BANK, 0, first=True)
            pe.wait_ge(supp_lo, T)
            pe.wait_ge(mix_in, T)
            edge(1, BANK, BANK, 1, first=True)
            with pe.Fori(2, NCH - 2, 2) as k0:
                for par in range(2):
                    edge(k0 + par, (k0 + par) * BANK, BANK, par)
            edge(NCH - 1, *CHUNKS[-1], 0)

            def score(p, c, first=False):
                if c >= SB or not first:
                    pe.wait_ge(scan_ok, PAIRS * p + c - SB + 1 if c >= SB else PAIRS * p - PAIRS + max(range(c, PAIRS, SB)) + 1)
                for n in range(2):
                    m = 2 * c + n
                    mm = split_product(pe, sc_bank[c % SB][:, n * 2 * P:(n + 1) * 2 * P],
                                       [[eh_t[q][:, j, m * P:(m + 1) * P] for j in range(KC)] for q in range(2)],
                                       [[eh_t[q][:, j, bass.ds(p * 2 * P, 2 * P)] for j in range(KC)] for q in range(2)])
                mm.then_inc(sc_mm, 1)

            def turn_max(p, first=False):
                pe.wait_ge(mx_ok, (PAIRS - 1) * (p + 1))
                if not first:
                    pe.wait_ge(negm_ok, p)
                for n in range(2):
                    for u in range(2):
                        tr = nc.tensor.transpose(mx_bank[:, (2 * u + n) * P:(2 * u + n + 1) * P],
                                                 run_max[:, (2 * n + u) * P:(2 * n + u + 1) * P], ident[:, :])
                tr.then_inc(mxt_mm, 1)

            def spread_max(p, par, first=False):
                pe.wait_ge(negm_ok, p + 1)
                if not first:
                    pe.wait_ge(sub_ok, 2 * p)
                for u in range(2):
                    tr = nc.tensor.transpose(bc_bank[:, u * P:(u + 1) * P],
                                             negm[:, par, u:u + 1].broadcast_to([P, P]), ident[:, :])
                tr.then_inc(bc_mm, 1)

            ROW_STEPS = [(0, s, m) for m in range(T) for s in (s_hi, s_lo)] + [(1, s_hi, m) for m in range(T)]

            def rows_out(pair_no, u, start, end, first=False, final=False):
                t = 2 * pair_no + u
                for n in range(start, end):
                    if n == 0:
                        pe.wait_ge(p_hi, t + 1)
                        if not first:
                            pe.wait_ge(fin1, F1 * (t - 1))
                    if n == 2 * T:
                        if final:
                            pe.wait_ge(p_lo_last, 1)
                        else:
                            pe.wait_ge(p_lo, t + 1)
                    a, s, m = ROW_STEPS[n]
                    mm = nc.tensor.matmul(acc_b[u][:, 0:D + 1], num[:, u, a, m], s[:, m, 0:D + 1],
                                          start=(n == 0), stop=(n == 3 * T - 1))
                if end == 3 * T:
                    mm.then_inc(o_mm, 1)

            def pair(p, par, first=False, second=False, last=False):
                for c in range(PAIRS):
                    if not last:
                        score(p + 1, c)
                    a, z = 12 * c, 12 * (c + 1)
                    if a < 3 * T and not first:
                        rows_out(p - 1, 1, a, min(z, 3 * T), second)
                    if c == 0:
                        turn_max(p, first)
                    if c == 1:
                        spread_max(p, par, first)
                    if z > 3 * T and not last:
                        rows_out(p, 0, max(a - 3 * T, 0), z - 3 * T, first)

            F1 = 3
            for c in range(PAIRS):
                pe.wait_ge(edge_lo, KC if c < 2 else KC * NCH)
                score(0, c, True)
            pe.wait_ge(ones_ok, 2)
            pair(0, 0, first=True)
            pair(1, 1, second=True)
            with pe.Fori(2, PAIRS - 2, 2) as p0:
                for n in range(2):
                    pair(p0 + n, n)
            pair(PAIRS - 1, 0, last=True)
            rows_out(PAIRS - 1, 0, 0, 2 * T)
            rows_out(PAIRS - 1, 1, 0, 2 * T)
            rows_out(PAIRS - 1, 0, 2 * T, 3 * T)
            rows_out(PAIRS - 1, 1, 2 * T, 3 * T, final=True)


_INS = ['x', 'adj', 'L0_gnn_W_sa', 'L0_gnn_a_sa', 'L0_gnn_W_gcnb', 'L0_gnn_b_gcnb', 'L0_gnn_Wa', 'L0_gnn_ba',
        'L0_gnn_Wb', 'L0_gnn_bb', 'L1_gnn_weight', 'L1_gnn_bias', 'L1_gnn_node_w', 'L1_gnn_edge_w']


def kernel(**inputs):
    import numpy as _np
    import concourse.bacc as _bacc
    from concourse import mybir as _mybir
    from concourse.bass_utils import run_bass_kernel_spmd as _run

    nc = _bacc.Bacc("TRN2", target_bir_lowering=False, num_devices=1)
    arrays, args = {}, []
    for name in _INS:
        a = _np.ascontiguousarray(inputs[name])
        arrays[f"in_{name}"] = a
        args.append(nc.dram_tensor(f"in_{name}", a.shape, _mybir.dt.from_np(a.dtype), kind="ExternalInput").ap())
    out = nc.dram_tensor("out_x", inputs['x'].shape, _mybir.dt.float32, kind="ExternalOutput").ap()
    build(nc, *args, out)
    r = _run(nc, [arrays], core_ids=[0])
    return r.results[0]["out_x"]
```
